# Optimizing a Trainium2 kernel written in Bass

```python
import numpy as np
import jax
import jax.numpy as jnp

def _softmax(x, axis=-1):
    return jax.nn.softmax(x, axis=axis)

def _gelu(x):
    return jax.nn.gelu(x, approximate=True)

def _silu(x):
    return jax.nn.silu(x)

def _sigmoid(x):
    return jax.nn.sigmoid(x)

def _layernorm(x, axis=-1, eps=1e-05):
    m = jnp.mean(x, axis=axis, keepdims=True)
    v = jnp.var(x, axis=axis, keepdims=True)
    return (x - m) / jnp.sqrt(v + eps)

def _scatter_add(tgt, idx, src, axis=0):
    return tgt.at[idx].add(src)

def _segment_sum(src, seg, n):
    return jax.ops.segment_sum(src, seg, n)
kernel_name = 'mk_seq_postln_d1_jaxref_r4_b4b142'

def setup_inputs(seed: int=0):
    np.random.seed(seed)
    _w = jnp.asarray

    def _L0_attn_setup():
        import math
        import jax, jax.numpy as jnp
        import numpy as np
        from jax import lax
        D_MODEL = 256
        N_LAYERS = 2
        D_STATE = 16
        D_CONV = 4
        EXPAND = 2
        D_INNER = EXPAND * D_MODEL
        DT_RANK = math.ceil(D_MODEL / 16)
        BATCH = 2
        SEQLEN = 256
        BETA = 0.6
        ALPHA = 1.0
        EPS = 1e-05
        DT_MIN, DT_MAX, DT_FLOOR = (0.001, 0.1, 0.0001)

        def _rmsnorm(x, w):
            return x * jax.lax.rsqrt(jnp.mean(x * x, axis=-1, keepdims=True) + EPS) * w

        def _block(x, in_w, cw, cb, xp_w, dtw, dtb, a_log, dp, ow):
            B, L, _ = x.shape
            xz = jnp.einsum('bld,ed->ble', x, in_w)
            xb, z = jnp.split(xz, 2, axis=-1)
            xc = lax.conv_general_dilated(xb.transpose(0, 2, 1), cw[:, None, :], window_strides=(1,), padding=[(D_CONV - 1, 0)], dimension_numbers=('NCH', 'OIH', 'NCH'), feature_group_count=D_INNER)
            xb = jax.nn.silu((xc + cb[None, :, None]).transpose(0, 2, 1))
            dbc = jnp.einsum('ble,re->blr', xb, xp_w)
            delta = dbc[..., :DT_RANK]
            Bm = dbc[..., DT_RANK:DT_RANK + D_STATE]
            Cm = dbc[..., DT_RANK + D_STATE:]
            delta = jax.nn.softplus(jnp.einsum('blr,er->ble', delta, dtw) + dtb)
            dA = jnp.exp(delta[..., None] * -jnp.exp(a_log))
            mi = ALPHA * delta[..., None] * Bm[:, :, None, :] * xb[..., None]

            def scan_fn(carry, inp):
                h, v = carry
                dA_t, mi_t, C_t = inp
                v = BETA * v + mi_t
                h = dA_t * h + v
                y_t = jnp.einsum('ben,bn->be', h, C_t)
                return ((h, v), y_t)
            h0 = jnp.zeros((B, D_INNER, D_STATE), dtype=x.dtype)
            _, ys = lax.scan(scan_fn, (h0, h0), (dA.transpose(1, 0, 2, 3), mi.transpose(1, 0, 2, 3), Cm.transpose(1, 0, 2)))
            y = ys.transpose(1, 0, 2) + dp * xb
            y = y * jax.nn.silu(z)
            return jnp.einsum('ble,de->bld', y, ow)
        key = jax.random.key(seed)
        ks = jax.random.split(key, 10)
        std = 0.02
        nl = N_LAYERS
        x = jax.random.normal(ks[0], (BATCH, SEQLEN, D_MODEL), dtype=jnp.float32)
        in_proj_w = jax.random.normal(ks[1], (nl, 2 * D_INNER, D_MODEL), dtype=jnp.float32) * std
        conv_w = jax.random.normal(ks[2], (nl, D_INNER, D_CONV), dtype=jnp.float32) * std
        conv_b = jnp.zeros((nl, D_INNER), dtype=jnp.float32)
        x_proj_w = jax.random.normal(ks[3], (nl, DT_RANK + 2 * D_STATE, D_INNER), dtype=jnp.float32) * std
        dt_std = DT_RANK ** (-0.5)
        dt_w = jax.random.uniform(ks[4], (nl, D_INNER, DT_RANK), dtype=jnp.float32, minval=-dt_std, maxval=dt_std)
        dt = jnp.exp(jax.random.uniform(ks[5], (nl, D_INNER), dtype=jnp.float32) * (math.log(DT_MAX) - math.log(DT_MIN)) + math.log(DT_MIN))
        dt = jnp.clip(dt, DT_FLOOR, None)
        dt_b = dt + jnp.log(-jnp.expm1(-dt))
        A_log = jnp.broadcast_to(jnp.log(jnp.arange(1, D_STATE + 1, dtype=jnp.float32)), (nl, D_INNER, D_STATE)).copy()
        Dp = jnp.ones((nl, D_INNER), dtype=jnp.float32)
        out_w = jax.random.normal(ks[6], (nl, D_MODEL, D_INNER), dtype=jnp.float32) * std
        norm_w = jnp.ones((nl, D_MODEL), dtype=jnp.float32)
        return {'x': x, 'norm_w': norm_w, 'in_proj_w': in_proj_w, 'conv_w': conv_w, 'conv_b': conv_b, 'x_proj_w': x_proj_w, 'dt_w': dt_w, 'dt_b': dt_b, 'A_log': A_log, 'Dp': Dp, 'out_w': out_w}
    _L0_attn_in = _L0_attn_setup()

    def _L0_ffn_setup():
        import jax, jax.numpy as jnp
        import numpy as np
        N_EXPERT_CAPACITY = 2
        key = jax.random.key(seed)
        k1, k2, k3, k4 = jax.random.split(key, 4)
        B, S, D, E, F = (8, 256, 256, 8, 512)
        x = jax.random.normal(k1, (B, S, D), dtype=jnp.float32)
        choice_w = jax.random.uniform(k2, (E, D), dtype=jnp.float32, minval=-1.0, maxval=1.0) * (1.0 / np.sqrt(D))
        w1 = jax.random.uniform(k3, (E, D, F), dtype=jnp.float32, minval=-1.0, maxval=1.0) * (1.0 / np.sqrt(D))
        w2 = jax.random.uniform(k4, (E, F, D), dtype=jnp.float32, minval=-1.0, maxval=1.0) * (1.0 / np.sqrt(F))
        return {'x': x, 'choice_w': choice_w, 'w1': w1, 'w2': w2}
    _L0_ffn_in = _L0_ffn_setup()
    _d = {'L0_attn_x': _L0_attn_in['x'], 'L0_attn_norm_w': _L0_attn_in['norm_w'], 'L0_attn_in_proj_w': _L0_attn_in['in_proj_w'], 'L0_attn_conv_w': _L0_attn_in['conv_w'], 'L0_attn_conv_b': _L0_attn_in['conv_b'], 'L0_attn_x_proj_w': _L0_attn_in['x_proj_w'], 'L0_attn_dt_w': _L0_attn_in['dt_w'], 'L0_attn_dt_b': _L0_attn_in['dt_b'], 'L0_attn_A_log': _L0_attn_in['A_log'], 'L0_attn_Dp': _L0_attn_in['Dp'], 'L0_attn_out_w': _L0_attn_in['out_w'], 'L0_ffn_choice_w': _L0_ffn_in['choice_w'], 'L0_ffn_w1': _L0_ffn_in['w1'], 'L0_ffn_w2': _L0_ffn_in['w2']}
    _x0 = _d['L0_attn_x']
    _d['L0_attn_x'] = jax.random.normal(jax.random.fold_in(jax.random.key(seed), 1), (1, 4096, 256), dtype=_x0.dtype)
    del _x0
    return _d

def reference(L0_attn_x, L0_attn_norm_w, L0_attn_in_proj_w, L0_attn_conv_w, L0_attn_conv_b, L0_attn_x_proj_w, L0_attn_dt_w, L0_attn_dt_b, L0_attn_A_log, L0_attn_Dp, L0_attn_out_w, L0_ffn_choice_w, L0_ffn_w1, L0_ffn_w2):

    def _L0_attn_ref(x, norm_w, in_proj_w, conv_w, conv_b, x_proj_w, dt_w, dt_b, A_log, Dp, out_w):
        import math
        import jax, jax.numpy as jnp
        import numpy as np
        from jax import lax
        D_MODEL = 256
        N_LAYERS = 2
        D_STATE = 16
        D_CONV = 4
        EXPAND = 2
        D_INNER = EXPAND * D_MODEL
        DT_RANK = math.ceil(D_MODEL / 16)
        BATCH = 2
        SEQLEN = 256
        BETA = 0.6
        ALPHA = 1.0
        EPS = 1e-05
        DT_MIN, DT_MAX, DT_FLOOR = (0.001, 0.1, 0.0001)

        def _rmsnorm(x, w):
            return x * jax.lax.rsqrt(jnp.mean(x * x, axis=-1, keepdims=True) + EPS) * w

        def _block(x, in_w, cw, cb, xp_w, dtw, dtb, a_log, dp, ow):
            B, L, _ = x.shape
            xz = jnp.einsum('bld,ed->ble', x, in_w)
            xb, z = jnp.split(xz, 2, axis=-1)
            xc = lax.conv_general_dilated(xb.transpose(0, 2, 1), cw[:, None, :], window_strides=(1,), padding=[(D_CONV - 1, 0)], dimension_numbers=('NCH', 'OIH', 'NCH'), feature_group_count=D_INNER)
            xb = jax.nn.silu((xc + cb[None, :, None]).transpose(0, 2, 1))
            dbc = jnp.einsum('ble,re->blr', xb, xp_w)
            delta = dbc[..., :DT_RANK]
            Bm = dbc[..., DT_RANK:DT_RANK + D_STATE]
            Cm = dbc[..., DT_RANK + D_STATE:]
            delta = jax.nn.softplus(jnp.einsum('blr,er->ble', delta, dtw) + dtb)
            dA = jnp.exp(delta[..., None] * -jnp.exp(a_log))
            mi = ALPHA * delta[..., None] * Bm[:, :, None, :] * xb[..., None]

            def scan_fn(carry, inp):
                h, v = carry
                dA_t, mi_t, C_t = inp
                v = BETA * v + mi_t
                h = dA_t * h + v
                y_t = jnp.einsum('ben,bn->be', h, C_t)
                return ((h, v), y_t)
            h0 = jnp.zeros((B, D_INNER, D_STATE), dtype=x.dtype)
            _, ys = lax.scan(scan_fn, (h0, h0), (dA.transpose(1, 0, 2, 3), mi.transpose(1, 0, 2, 3), Cm.transpose(1, 0, 2)))
            y = ys.transpose(1, 0, 2) + dp * xb
            y = y * jax.nn.silu(z)
            return jnp.einsum('ble,de->bld', y, ow)
        for i in range(N_LAYERS):
            x = x + _block(_rmsnorm(x, norm_w[i]), in_proj_w[i], conv_w[i], conv_b[i], x_proj_w[i], dt_w[i], dt_b[i], A_log[i], Dp[i], out_w[i])
        return x

    def _L0_ffn_ref(x, choice_w, w1, w2):
        import jax, jax.numpy as jnp
        import numpy as np
        N_EXPERT_CAPACITY = 2
        B, S, D = x.shape
        E = choice_w.shape[0]
        k = S * N_EXPERT_CAPACITY // E
        probs = jax.nn.softmax(jnp.einsum('bsd,ed->bse', x, choice_w), axis=-1)
        G, I = jax.lax.top_k(jnp.swapaxes(probs, -1, -2), k)
        x_in = jnp.take_along_axis(x[:, None, :, :], I[..., None], axis=2)
        h = jax.nn.silu(jnp.einsum('bekd,edf->bekf', x_in, w1))
        x_mlp = jnp.einsum('bekf,efd->bekd', h, w2)
        b_idx = jnp.arange(B)[:, None, None]
        out = jnp.zeros_like(x).at[b_idx, I].add(G[..., None] * x_mlp)
        return out
    x = L0_attn_x
    x = _layernorm(x + _L0_attn_ref(x, L0_attn_norm_w, L0_attn_in_proj_w, L0_attn_conv_w, L0_attn_conv_b, L0_attn_x_proj_w, L0_attn_dt_w, L0_attn_dt_b, L0_attn_A_log, L0_attn_Dp, L0_attn_out_w), axis=-1)
    x = _layernorm(x + _L0_ffn_ref(x, L0_ffn_choice_w, L0_ffn_w1, L0_ffn_w2), axis=-1)
    return x

_drawn_inputs = setup_inputs


def setup_inputs(seed=0):
    import zlib

    import numpy as np

    out = dict(_drawn_inputs(seed))
    spreads = {'L0_attn_norm_w': (1.0, 0.6), 'L0_attn_conv_b': (0.0, 0.8), 'L0_attn_Dp': (1.0, 0.6)}
    factors = {'L0_attn_in_proj_w': 8.0,
     'L0_attn_conv_w': 8.0,
     'L0_attn_x_proj_w': 8.0,
     'L0_attn_dt_w': 8.0,
     'L0_attn_dt_b': 8.0,
     'L0_attn_A_log': 8.0,
     'L0_attn_out_w': 8.0}
    for name, (base, spread) in spreads.items():
        noise = np.random.default_rng([zlib.crc32(name.encode()), seed]).standard_normal(out[name].shape)
        drawn = base * np.exp(spread * noise) if base else spread * noise
        out[name] = jnp.asarray(drawn.astype(out[name].dtype))
    for name, factor in factors.items():
        out[name] = (out[name] * factor).astype(out[name].dtype)
    return out
```

```python
from contextlib import ExitStack

import concourse.bass as bass
from concourse import mybir

F32 = mybir.dt.float32
BF16 = mybir.dt.bfloat16
U32 = mybir.dt.uint32
ALU = mybir.AluOpType
ACT = mybir.ActivationFunctionType
AXX = mybir.AxisListType.X

P = 128
T = 4096
D = 256
DK = D // P
E = 512
ET = E // P
N = 16
R = 16
TAPS = 4
BETA = 0.6
EPS = 1e-5
NL = 2
TC = 256
NC = T // TC
BT = 64
NB = TC // BT
TJ = TC // P
KV = BT + N
HN = 8
NU = ET * NB
DBC = 80
B_ROW, C_ROW = 32, 64
U_FLOOR = 2.0 ** -80
PROJ = 7
RING = 4

P_NORM = 0
P_CW = P_NORM + DK
P_CB = P_CW + ET * TAPS
P_DTB = P_CB + ET
P_DP = P_DTB + ET
P_ALL = P_DP + ET

NX = 8
CAP = T * 2 // NX
F = 512
FK = F // P
TT = T // P
CG = CAP // P
GRP = 8
NG = TT // GRP
VALS = 5
BITS = 30


def take_waits(eng, waited):
    eng.sem_inc(waited, 1)


def unit(u):
    pair, rest = divmod(u, 2 * NB)
    b, e = divmod(rest, 2)
    return pair, b, e, 2 * pair + e


def build_mamba(nc, ins, seq):
    with ExitStack() as ctx:
        def sb(name, shape, dt=F32):
            return ctx.enter_context(nc.sbuf_tensor(name, shape, dt))

        def ps(name, shape, dt=F32):
            return ctx.enter_context(nc.psum_tensor(name, shape, dt))

        def sem(name):
            return ctx.enter_context(nc.semaphore(name))

        c_dram = nc.dram_tensor("c_rows", [2, NB, N, BT], F32, kind="Internal").ap()

        w_in = sb("w_in", [P, DK, 2 * E])
        w_out = sb("w_out", [P, ET, D])
        w_xp = sb("w_xp", [P, ET, DBC])
        w_dt = sb("w_dt", [R, E])
        prm = sb("prm", [P, P_ALL])
        rate = sb("rate", [P, ET, N])
        ident = sb("ident", [P, P])
        tri = sb("tri", [BT, BT])
        zcol = sb("zcol", [P, NB * N])
        ssq = sb("ssq", [P, TT])
        rstd = sb("rstd", [P, TT])
        x_in = sb("x_in", [P, TJ, D])
        tmp1 = sb("tmp1", [P, ET * TC])
        xn = tmp1[:, 0:TJ * D].rearrange("p (j d) -> p j d", j=TJ)
        xnT = tmp1[:, TJ * D:TJ * D + DK * TC].rearrange("p (k t) -> p k t", k=DK)
        t1 = tmp1[:, :].rearrange("p (e t) -> p e t", e=ET)
        tmp3 = sb("tmp3", [P, ET * (TC + TAPS - 1)])
        xb = tmp3[:, :].rearrange("p (e t) -> p e t", e=ET)
        t3 = tmp3[:, 0:ET * TC].rearrange("p (e t) -> p e t", e=ET)
        eps_col = sb("eps_col", [P, 1])
        one_col = sb("one_col", [P, 1])
        halo = sb("halo", [P, ET, TAPS - 1])
        xc = [sb(f"xc{q}", [P, ET, TC]) for q in range(2)]
        sz = [sb(f"sz{q}", [P, ET, TC]) for q in range(2)]
        dl = [sb(f"dl{q}", [P, ET, TC]) for q in range(2)]
        dbc = sb("dbc", [DBC, TC])
        mv = [[sb(f"mv{q}{b}", [KV, N, BT]) for b in range(NB)] for q in range(2)]
        ut = [[sb(f"ut{q}{b}", [KV, E]) for b in range(NB)] for q in range(2)]
        da = [sb(f"da{e}", [P, NB, N, BT]) for e in range(ET)]
        a0 = [sb(f"a0{e}", [P, NB, N]) for e in range(ET)]
        cb = sb("cb", [P, NB, N * BT])
        ht = [sb(f"ht{r}", [P, N * BT]) for r in range(RING)]
        first = sb("first", [P, ET, N])
        hlast = sb("hlast", [P, ET, N])
        y = [sb(f"y{q}", [P, ET, TC]) for q in range(2)]
        xo = sb("xo", [P, TJ, D])

        pv = [ps(f"pv{s}", [P, N, BT]) for s in range(2)]
        pp = [ps(f"pp{s}", [P, 2, TC]) for s in range(2)]
        pT = ps("pT", [P, 512])
        pC = ps("pC", [P, 512])

        s = {n: sem("s_" + n) for n in (
            "x_copied", "const_loaded", "x0_loaded", "ssq_done", "w_loaded", "sqrt_done", "rstd_done",
            "rate", "zeroed", "x_loaded", "xn_done", "xT_done", "xnT_done", "halo_done", 
            "proj_done", "proj_read", "tap0_done", "tap_done", "xc_done",   "z_done",
            "w1_done", "corr_done", "ln_done", "sum_done", "dl_done", "u_done", "bT_done", "m_done",
            "uT_done", "ut_done", "carry_done", "cr_done", "c_stored", "exp_done", "a0_copied",
            "a_done", "v_done", "first_done", "add_done", "scan_done", "h_done", "p_done", "y_done",
            "ydp_done", "gate_done", "out_done", "xo_loaded", "xo_done", "xo_stored", "sq_done",
            "halo_set", "waited_sp", "waited_pe")}
        cb_loaded = [sem(f"cb_loaded{b}") for b in range(NB)]

        block = ctx.enter_context(nc.Block())

        def layers(eng, prologue, front, main, post):
            with eng.Fori(0, NL) as l:
                prologue(l)
                front(l * NC, 0, 0)
                main(l * NC, 0, 0)
                with eng.Fori(0, (NC - 2) // 2) as i:
                    for j in range(2):
                        main(l * NC + 2 * i + 1 + j, 1 + j, 2 * i + 1 + j)
                main(l * NC + NC - 1, NC - 1, NC - 1)
                post(l * NC + NC - 1, NC - 1, NC - 1)

        def slots(items, g, c, cc):
            table = {}
            for slot, kind, f in items:
                if kind == "front" and c != NC - 1:
                    table.setdefault(slot, []).append(lambda f=f: f(g + 1, c + 1, cc + 1))
                if kind == "back" and c != 0:
                    table.setdefault(slot, []).append(lambda f=f: f(g - 1, c - 1, cc - 1))
            return table

        @block.sync
        def _(sp):
            sp.dma_start(seq[0:T, :], ins["x"]).then_inc(s["x_copied"], 16)
            sp.dma_start(ident[:], ins["ident"]).then_inc(s["const_loaded"], 16)
            sp.dma_start(tri[:], ins["tri"]).then_inc(s["const_loaded"], 16)
            for q in range(2):
                for b in range(NB):
                    sp.dma_start(mv[q][b][BT:KV, :, :], ins["carry"]).then_inc(s["const_loaded"], 16)
            sp.wait_ge(s["x_copied"], 16)

            def load_x(g, c, cc):
                if c:
                    sp.wait_ge(s["xn_done"], g)
                    take_waits(sp, s["waited_sp"])
                sp.dma_start(x_in[:], seq[bass.ds(g * TC, TC), :].rearrange(
                    "(j p) d -> p j d", p=P)).then_inc(s["x_loaded"], 16)

            def load_c(g, c, cc):
                q = c % 2
                sp.wait_ge(s["proj_read"], PROJ * g + 5)
                take_waits(sp, s["waited_sp"])
                sp.dma_start(c_dram[q].rearrange("b n t -> n b t"),
                             dbc[C_ROW:C_ROW + N, :].rearrange("n (b t) -> n b t", b=NB)
                             ).then_inc(s["c_stored"], 16)
                sp.wait_ge(s["c_stored"], 16 * g + 16)
                take_waits(sp, s["waited_sp"])
                for b in range(NB):
                    if c:
                        sp.wait_ge(s["p_done"], NU * (g - 1) + 2 * NB + 2 * b + 2)
                        take_waits(sp, s["waited_sp"])
                    sp.dma_start(cb[:, b, :], c_dram[q, b].rearrange("n t -> (n t)")
                                 .partition_broadcast(P)).then_inc(cb_loaded[b], 16)

            def load_xo(g, c, cc):
                if c:
                    sp.wait_ge(s["xo_stored"], 16 * g)
                    take_waits(sp, s["waited_sp"])
                    sp.wait_ge(s["sq_done"], g)
                    take_waits(sp, s["waited_sp"])
                sp.dma_start(xo[:], seq[bass.ds(g * TC, TC), :].rearrange(
                    "(j p) d -> p j d", p=P)).then_inc(s["xo_loaded"], 16)

            def store_xo(g, c, cc):
                sp.wait_ge(s["xo_done"], g + 1)
                take_waits(sp, s["waited_sp"])
                sp.dma_start(seq[bass.ds((g + NC) * TC, TC), :].rearrange(
                    "(j p) d -> p j d", p=P), xo[:]).then_inc(s["xo_stored"], 16)

            def prologue(l):
                sp.wait_ge(s["xo_stored"], l * (16 * NC))
                take_waits(sp, s["waited_sp"])
                sp.wait_ge(s["sq_done"], l * NC)
                take_waits(sp, s["waited_sp"])
                one = bass.ds(l, 1)
                for dst, name in ((w_in, "w_in"), (w_out, "w_out"), (w_xp, "w_xp")):
                    sp.dma_start(dst[:], ins[name][one].rearrange("a p k n -> p (a k) n")
                                 ).then_inc(s["w_loaded"], 16)
                sp.dma_start(w_dt[:], ins["w_dt"][one].rearrange("a r n -> r (a n)")
                             ).then_inc(s["w_loaded"], 16)
                sp.dma_start(prm[:], ins["prm"][one].rearrange("a p n -> p (a n)")
                             ).then_inc(s["w_loaded"], 16)
                sp.dma_start(rate[:], ins["a_log"][one].rearrange("a p e n -> p (a e) n")
                             ).then_inc(s["w_loaded"], 16)

            def main(g, c, cc):
                if c:
                    load_xo(g - 1, c - 1, None)
                if c < NC - 2:
                    load_x(g + 2, c + 2, None)
                if c:
                    store_xo(g - 1, c - 1, None)
                if c < NC - 1:
                    load_c(g + 1, c + 1, None)

            with sp.Fori(0, NL) as l:
                g0 = l * NC
                prologue(l)
                load_x(g0, 0, 0)
                load_x(g0 + 1, 1, 1)
                load_c(g0, 0, 0)
                main(g0, 0, 0)
                with sp.Fori(0, (NC - 4) // 2) as i:
                    for j in range(2):
                        main(g0 + 2 * i + 1 + j, 1 + j, None)
                for c in range(NC - 3, NC):
                    main(g0 + c, c, c)
                load_xo(g0 + NC - 1, NC - 1, NC - 1)
                store_xo(g0 + NC - 1, NC - 1, NC - 1)
            sp.wait_ge(s["xo_stored"], 16 * NC * NL)

        W_ALL = 16 * 6

        @block.scalar
        def _(act):
            xall = [da[e][:].rearrange("p b n t -> p (b n t)").rearrange("p (j d) -> p j d", d=D)
                    for e in range(2)]
            for h in range(2):
                act.dma_start(xall[h], ins["x"][bass.ds(h * (T // 2), T // 2), :].rearrange(
                    "(j p) d -> p j d", p=P)).then_inc(s["x0_loaded"], 16)
            for h in range(2):
                act.wait_ge(s["x0_loaded"], 16 * 2)
                for j in range(TT // 2):
                    n = h * (TT // 2) + j
                    if n >= 4:
                        act.wait_ge(s["ssq_done"], n - 3)
                    act.activation(tmp3[:, n % 4 * D:(n % 4 + 1) * D], xall[h][:, j, :], ACT.Square,
                                   accum_out=ssq[:, h * (TT // 2) + j:h * (TT // 2) + j + 1]
                                   ).then_inc(s["ssq_done"], 1)

            def prologue(l):
                act.wait_ge(s["ssq_done"], TT)
                act.wait_ge(s["sq_done"], l * NC)
                act.wait_ge(s["zeroed"], 1)
                act.activation(rstd[:], ssq[:], ACT.Sqrt, scale=1.0 / D, bias=eps_col[:, 0:1]
                               ).then_inc(s["sqrt_done"], 1)
                act.wait_ge(s["w_loaded"], W_ALL * (l + 1))
                act.activation(rate[:], rate[:], ACT.Exp).then_inc(s["rate"], 1)
                act.wait_ge(s["rate"], l + 1)

            def halo_front(g, c, cc):
                if c == 0:
                    act.wait_ge(s["zeroed"], 1)
                    act.activation(xb[:, :, 0:TAPS - 1], zcol[:, 0:ET * (TAPS - 1)].rearrange(
                        "p (e t) -> p e t", e=ET), ACT.Copy).then_inc(s["halo_done"], 1)
                else:
                    act.wait_ge(s["dl_done"], g)
                    act.wait_ge(s["halo_set"], g)
                    act.activation(xb[:, :, 0:TAPS - 1], halo[:], ACT.Copy).then_inc(s["halo_done"], 1)

            def xnT_scale(g, c, cc):
                act.wait_ge(s["xT_done"], g + 1)
                for k in range(DK):
                    act.activation(xnT[:, k, :], pT[:, k * TC:(k + 1) * TC], ACT.Copy,
                                   scale=prm[:, P_NORM + k:P_NORM + k + 1]).then_inc(s["xnT_done"], 1)

            def xb_copy(i):
                def f(g, c, cc):
                    slot = (PROJ * c + i) % 2
                    act.wait_ge(s["proj_done"], PROJ * g + i + 1)
                    act.activation(xb[:, 2 * i:2 * i + 2, TAPS - 1:TAPS - 1 + TC], pp[slot][:], ACT.Copy
                                   ).then_inc(s["proj_read"], 1)
                return f

            def z_silu(i):
                def f(g, c, cc):
                    q, slot = c % 2, (PROJ * c + 2 + i) % 2
                    if i == 0 and c:
                        act.wait_ge(s["gate_done"], g - 1)
                    act.wait_ge(s["proj_done"], PROJ * g + 3 + i)
                    act.activation(sz[q][:, 2 * i:2 * i + 2, :], pp[slot][:], ACT.Silu
                                   ).then_inc(s["proj_read"], 1)
                return f

            def conv_first(g, c, cc):
                act.wait_ge(s["proj_read"], PROJ * g + 2)
                act.wait_ge(s["halo_done"], g + 1)
                act.activation(halo[:], xb[:, :, TC:TC + TAPS - 1], ACT.Copy).then_inc(s["halo_set"], 1)
                act.wait_ge(s["proj_done"], PROJ * g + 4)
                for e in range(ET):
                    act.activation(t1[:, e, :], xb[:, e, 0:TC], ACT.Identity,
                                   scale=prm[:, P_CW + e * TAPS:P_CW + e * TAPS + 1],
                                   bias=prm[:, P_CB + e:P_CB + e + 1]).then_inc(s["tap0_done"], 1)

            def xc_silu(g, c, cc):
                q = c % 2
                act.wait_ge(s["tap_done"], ET * (TAPS - 1) * (g + 1))
                if c:
                    act.wait_ge(s["ydp_done"], ET * (g - 1))
                act.activation(xc[q][:], t1, ACT.Silu).then_inc(s["xc_done"], 1)

            def dbc_copy(g, c, cc):
                slot = (PROJ * c + 4) % 2
                act.wait_ge(s["proj_done"], PROJ * g + 5)
                if c:
                    act.wait_ge(s["c_stored"], 16 * g)
                act.activation(dbc[:], pp[slot][0:DBC, 0, :], ACT.Copy).then_inc(s["proj_read"], 1)

            def softplus_in(g, c, cc):
                q = c % 2
                if c:
                    act.wait_ge(s["exp_done"], ET * (g - 1))
                act.wait_ge(s["xc_done"], g + 1)
                for i in range(2):
                    slot = (PROJ * c + 5 + i) % 2
                    act.wait_ge(s["proj_done"], PROJ * g + 6 + i)
                    for e in range(2):
                        et = 2 * i + e
                        bias = prm[:, P_DTB + et:P_DTB + et + 1]
                        act.activation(t1[:, et, :], pp[slot][:, e, :], ACT.Abs, bias=bias)
                        last = act.activation(dl[q][:, et, :], pp[slot][:, e, :], ACT.Relu, bias=bias)
                    last.then_inc(s["proj_read"], 1)
                act.wait_ge(s["proj_read"], PROJ * (g + 1))
                act.activation(t1, t1, ACT.Exp, scale=-1.0).then_inc(s["z_done"], 1)
                act.wait_ge(s["z_done"], g + 1)
                act.activation(t3, t1, ACT.Identity, bias=one_col[:, 0:1]).then_inc(s["w1_done"], 1)

            def softplus_ln(g, c, cc):
                act.wait_ge(s["sum_done"], g + 1)
                act.wait_ge(s["w1_done"], g + 1)
                act.activation(t1, t3, ACT.Ln).then_inc(s["ln_done"], 1)

            def ut_copy(b):
                def f(g, c, cc):
                    q = c % 2
                    if b == 0 and c:
                        act.wait_ge(s["v_done"], NU * (g - 1))
                    act.wait_ge(s["uT_done"], NB * g + b + 1)
                    act.activation(ut[q][b][0:BT, :], pT[0:BT, :], ACT.Copy).then_inc(s["ut_done"], 1)
                return f

            def carry_copy(b):
                def f(g, c, cc):
                    q = c % 2
                    act.wait_ge(s["carry_done"], NB * g + b + 1)
                    if b < NB - 1:
                        dst = ut[q][b + 1]
                    else:
                        dst = ut[1 - q][0]
                        if c:
                            act.wait_ge(s["v_done"], NU * (g - 1) + 2 * NB + 2)
                    act.activation(dst[BT:KV, :], pC[0:N, :], ACT.Copy).then_inc(s["cr_done"], 1)
                return f

            def exps(et, n0, n1):
                def f(g, c, cc):
                    q = c % 2
                    if n0 == 0:
                        act.wait_ge(s["dl_done"], g + 1)
                        if c:
                            last = (et // 2) * 2 * NB + 2 * (NB - 1) + et % 2
                            act.wait_ge(s["scan_done"], NU * (g - 1) + last + 1)
                    for n in range(n0, n1):
                        ins_ = act.activation(da[et][:, :, n, :], dl[q][:, et, :].rearrange(
                            "p (b t) -> p b t", b=NB), ACT.Exp, scale=rate[:, et, n:n + 1])
                    if n1 == N:
                        ins_.then_inc(s["exp_done"], 1)
                        act.wait_ge(s["exp_done"], ET * g + et + 1)
                        act.activation(a0[et][:], da[et][:, :, :, 0], ACT.Copy).then_inc(s["a0_copied"], 1)
                        act.wait_ge(s["a0_copied"], ET * g + et + 1)
                        act.activation(da[et][:, :, :, 0], zcol[:].rearrange("p (b n) -> p b n", b=NB),
                                       ACT.Copy).then_inc(s["a_done"], 1)
                return f

            def square(g, c, cc):
                act.wait_ge(s["xo_done"], g + 1)
                for j in range(TJ):
                    i = act.activation(y[c % 2][:, j, :], xo[:, j, :], ACT.Square,
                                       accum_out=ssq[:, bass.ds(cc * TJ + j, 1)])
                i.then_inc(s["sq_done"], 1)

            def front(g, c, cc):
                for f in (xnT_scale, halo_front, xb_copy(0), xb_copy(1), conv_first, z_silu(0), z_silu(1),
                          xc_silu, dbc_copy, softplus_in, softplus_ln):
                    f(g, c, cc)
                for b in range(NB):
                    ut_copy(b)(g, c, cc)
                    carry_copy(b)(g, c, cc)
                exps(0, 0, N)(g, c, cc)
                exps(1, 0, N)(g, c, cc)

            items = [(0, "own", exps(2, 0, 8)),
                     (1, "front", xnT_scale),
                     (1, "own", exps(2, 8, N)),
                     (2, "front", halo_front),
                     (2, "front", xb_copy(0)), (3, "front", xb_copy(1)),
                     (3, "front", conv_first),
                     (3, "own", exps(3, 0, 4)),
                     (4, "front", z_silu(0)), (4, "front", z_silu(1)),
                     (5, "front", xc_silu),
                     (5, "own", exps(3, 4, 8)),
                     (6, "front", dbc_copy),
                     (6, "own", exps(3, 8, N)),
                     (7, "front", softplus_in),
                     (8, "back", square),
                     (8, "front", softplus_ln),
                     (11, "front", exps(0, 0, 8)),
                     (11, "front", ut_copy(0)), (11, "front", carry_copy(0)),
                     (12, "front", exps(0, 8, N)),
                     (12, "front", ut_copy(1)), (12, "front", carry_copy(1)),
                     (13, "front", exps(1, 0, 8)),
                     (13, "front", ut_copy(2)), (13, "front", carry_copy(2)),
                     (14, "front", exps(1, 8, N)),
                     (14, "front", ut_copy(3)), (14, "front", carry_copy(3))]

            def main(g, c, cc):
                for slot, kind, f in items:
                    if kind == "own":
                        f(g, c, cc)
                    elif kind == "front" and c != NC - 1:
                        f(g + 1, c + 1, cc + 1)
                    elif kind == "back" and c:
                        f(g - 1, c - 1, cc - 1)

            layers(act, prologue, front, main, square)

        @block.tensor
        def _(pe):
            pe.wait_ge(s["const_loaded"], 16 * (2 + 2 * NB))

            def prologue(l):
                pe.wait_ge(s["w_loaded"], W_ALL * (l + 1))
                pe.wait_ge(s["zeroed"], 3 * l + 4)

            def x_transpose(g, c, cc):
                pe.wait_ge(s["xn_done"], g + 1)
                if c:
                    pe.wait_ge(s["ut_done"], NB * g)
                for k in range(DK):
                    for j in range(TJ):
                        i = pe.transpose(pT[:, k * TC + j * P:k * TC + (j + 1) * P],
                                         xn[:, j, k * P:(k + 1) * P], ident[:])
                i.then_inc(s["xT_done"], 1)

            def proj_slot(g, c, i):
                n = PROJ * g + i - 1
                if c or i >= 2:
                    pe.wait_ge(s["proj_read"], n)
                return (PROJ * c + i) % 2

            def in_proj(i):
                def f(g, c, cc):
                    slot = proj_slot(g, c, i)
                    if i == 0:
                        pe.wait_ge(s["xnT_done"], DK * (g + 1))
                    for e in range(2):
                        m = (2 * i + e) * P
                        for k in range(DK):
                            mm = pe.matmul(pp[slot][:, e, :], w_in[:, k, m:m + P], xnT[:, k, :],
                                           start=(k == 0), stop=(k == DK - 1))
                    mm.then_inc(s["proj_done"], 1)
                return f

            def x_proj(g, c, cc):
                q, slot = c % 2, proj_slot(g, c, 4)
                pe.wait_ge(s["xc_done"], g + 1)
                for e in range(ET):
                    mm = pe.matmul(pp[slot][0:DBC, 0, :], w_xp[:, e, :], xc[q][:, e, :],
                                   start=(e == 0), stop=(e == ET - 1))
                mm.then_inc(s["proj_done"], 1)

            def dt_proj(g, c, cc):
                pe.wait_ge(s["proj_read"], PROJ * g + 5)
                for i in range(2):
                    slot = proj_slot(g, c, 5 + i)
                    for e in range(2):
                        m = (2 * i + e) * P
                        mm = pe.matmul(pp[slot][:, e, :], w_dt[:, m:m + P], dbc[0:R, :],
                                       start=True, stop=True)
                    mm.then_inc(s["proj_done"], 1)

            def b_transpose(g, c, cc):
                if c:
                    pe.wait_ge(s["cr_done"], NB * g)
                    pe.wait_ge(s["xo_done"], g - 1)
                    take_waits(pe, s["waited_pe"])
                for b in range(NB):
                    mm = pe.transpose(pC[0:BT, b * DBC:(b + 1) * DBC], dbc[:, b * BT:(b + 1) * BT],
                                      ident[0:DBC, 0:DBC])
                mm.then_inc(s["bT_done"], 1)

            def u_transpose(b):
                def f(g, c, cc):
                    if b == 0:
                        pe.wait_ge(s["u_done"], g + 1)
                        pe.wait_ge(s["xnT_done"], DK * (g + 1))
                    else:
                        pe.wait_ge(s["ut_done"], NB * g + b)
                    take_waits(pe, s["waited_pe"])
                    for e in range(ET):
                        mm = pe.transpose(pT[0:BT, e * P:(e + 1) * P], t1[:, e, b * BT:(b + 1) * BT],
                                          ident[:])
                    mm.then_inc(s["uT_done"], 1)
                return f

            def carry(b):
                def f(g, c, cc):
                    q = c % 2
                    pe.wait_ge(s["m_done"], NB * (g + 1))
                    pe.wait_ge(s["ut_done"], NB * g + b + 1)
                    if c or b:
                        pe.wait_ge(s["cr_done"], NB * g + b)
                    pe.matmul(pC[0:N, :], mv[q][b][:, :, BT - 1], ut[q][b][:], start=True, stop=True
                              ).then_inc(s["carry_done"], 1)
                return f

            def v_unit(g, c, u):
                q = c % 2
                _, b, _, et = unit(u)
                if c or u >= 2:
                    pe.wait_ge(s["scan_done"], NU * g + u - 1)
                if u == 0 and c == 0:
                    pe.wait_ge(s["cr_done"], NB * (g + 1))
                for h in range(N // HN):
                    mm = pe.matmul(pv[u % 2][:, h * HN:(h + 1) * HN, :], ut[q][b][:, et * P:(et + 1) * P],
                                   mv[q][b][:, h * HN:(h + 1) * HN, :], start=True, stop=True)
                mm.then_inc(s["v_done"], 1)

            def out_proj(g, c, cc):
                q = c % 2
                pe.wait_ge(s["gate_done"], g + 1)
                for j in range(TJ):
                    for e in range(ET):
                        mm = pe.matmul(pC[:, j * D:(j + 1) * D], y[q][:, e, j * P:(j + 1) * P],
                                       w_out[:, e, :], start=(e == 0), stop=(e == ET - 1))
                mm.then_inc(s["out_done"], 1)

            def out_proj_main(g, c, cc):
                pe.wait_ge(s["cr_done"], NB * (g + 2))
                out_proj(g, c, cc)

            def front(g, c, cc):
                for f in (x_transpose, in_proj(0), in_proj(1), in_proj(2), in_proj(3), x_proj, dt_proj,
                          b_transpose):
                    f(g, c, cc)
                for b in range(NB):
                    u_transpose(b)(g, c, cc)
                    carry(b)(g, c, cc)

            items = [(1, "front", x_transpose),
                     (2, "front", in_proj(0)), (3, "front", in_proj(1)),
                     (4, "front", in_proj(2)), (5, "front", in_proj(3)),
                     (6, "back", out_proj_main),
                     (7, "front", x_proj), (8, "front", dt_proj), (8, "front", b_transpose),
                     (11, "front", u_transpose(0)), (12, "front", carry(0)),
                     (12, "front", u_transpose(1)), (13, "front", carry(1)),
                     (13, "front", u_transpose(2)), (14, "front", carry(2)),
                     (14, "front", u_transpose(3)), (15, "front", carry(3))]

            def main(g, c, cc):
                table = slots(items, g, c, cc)
                for u in range(NU):
                    for f in table.get(u, []):
                        f()
                    v_unit(g, c, u)

            def post(g, c, cc):
                pe.wait_ge(s["xo_done"], g)
                out_proj(g, c, cc)

            layers(pe, prologue, front, main, post)

        @block.vector
        def _(dve):
            dve.memset(eps_col[:], EPS)
            dve.memset(one_col[:], 1.0)
            dve.memset(zcol[:], 0.0).then_inc(s["zeroed"], 1)

            def prologue(l):
                dve.wait_ge(s["sqrt_done"], l + 1)
                dve.reciprocal(rstd[:], rstd[:]).then_inc(s["rstd_done"], 1)
                dve.memset(ut[0][0][BT:KV, :], 0.0).then_inc(s["zeroed"], 1)
                dve.memset(first[:], 0.0).then_inc(s["zeroed"], 1)
                dve.memset(hlast[:], 0.0).then_inc(s["zeroed"], 1)
                dve.wait_ge(s["rstd_done"], l + 1)
                dve.wait_ge(s["zeroed"], 3 * l + 4)

            def x_norm(g, c, cc):
                dve.wait_ge(s["x_loaded"], 16 * (g + 1))
                if c:
                    dve.wait_ge(s["uT_done"], NB * g)
                for j in range(TJ):
                    i = dve.tensor_scalar(xn[:, j, :], x_in[:, j, :], rstd[:, bass.ds(cc * TJ + j, 1)],
                                          None, ALU.mult)
                i.then_inc(s["xn_done"], 1)

            def conv(g, c, cc):
                for k in range(1, TAPS):
                    for e in range(ET):
                        n = ET * (TAPS - 1) * g + ET * (k - 1) + e
                        if k == 1:
                            dve.wait_ge(s["tap0_done"], ET * g + e + 1)
                        else:
                            dve.wait_ge(s["tap_done"], n - ET + 1)
                        w = P_CW + e * TAPS + k
                        dve.scalar_tensor_tensor(t1[:, e, :], xb[:, e, k:k + TC], prm[:, w:w + 1],
                                                 t1[:, e, :], ALU.mult, ALU.add).then_inc(s["tap_done"], 1)

            def step_size(g, c, cc):
                q = c % 2
                dve.wait_ge(s["ln_done"], g + 1)
                dve.scalar_tensor_tensor(t3, t3, -1.0, t1, ALU.add, ALU.subtract
                                         ).then_inc(s["corr_done"], 1)
                dve.wait_ge(s["corr_done"], g + 1)
                dve.scalar_tensor_tensor(dl[q][:], t3, 0.0, dl[q][:], ALU.max, ALU.subtract
                                         ).then_inc(s["dl_done"], 1)
                dve.wait_ge(s["dl_done"], g + 1)
                dve.scalar_tensor_tensor(t1, dl[q][:], -U_FLOOR, xc[q][:], ALU.min, ALU.mult
                                         ).then_inc(s["u_done"], 1)

            def moving(b):
                def f(g, c, cc):
                    q = c % 2
                    if b == 0:
                        dve.wait_ge(s["bT_done"], g + 1)
                        if c:
                            dve.wait_ge(s["v_done"], NU * (g - 1))
                    bT = pC[0:BT, b * DBC + B_ROW:b * DBC + B_ROW + N]
                    dve.tensor_tensor(mv[q][b][0:BT, :, :],
                                      tri[:].rearrange("p (o t) -> p o t", o=1).broadcast_to([BT, N, BT]),
                                      bT.rearrange("p (n o) -> p n o", o=1).broadcast_to([BT, N, BT]),
                                      ALU.mult).then_inc(s["m_done"], 1)
                return f

            def sum_n(g, c, u):
                q = c % 2
                _, b, _, et = unit(u)
                if u == 0 and c:
                    dve.wait_ge(s["out_done"], g - 1)
                    dve.wait_ge(s["sq_done"], g - 1)
                dve.wait_ge(s["p_done"], NU * g + u + 1)
                dve.tensor_reduce(y[q][:, et, b * BT:(b + 1) * BT],
                                  ht[u % RING][:].rearrange("p (n t) -> p t n", n=N),
                                  AXX, ALU.add).then_inc(s["y_done"], 1)

            def scan_unit(g, c, u):
                _, b, e, et = unit(u)
                h = ht[u % RING]
                a = da[et][:, b, :, :].rearrange("p n t -> p (n t)")
                if b == 0:
                    dve.wait_ge(s["a_done"], ET * g + et + 1)
                    if c:
                        dve.wait_ge(s["h_done"], NU * (g - 1) + (et // 2) * 2 * NB + 2 * (NB - 1) + e + 1)
                    dve.tensor_tensor(first[:, et, :], a0[et][:, 0, :], hlast[:, et, :], ALU.mult
                                      ).then_inc(s["first_done"], 1)
                    dve.wait_ge(s["first_done"], ET * g + et + 1)
                else:
                    dve.wait_ge(s["h_done"], NU * g + u - 1)
                dve.wait_ge(s["v_done"], NU * g + u + 1)
                v0 = pv[u % 2][:, :, 0]
                dve.tensor_tensor(v0, v0, first[:, et, :], ALU.add).then_inc(s["add_done"], 1)
                dve.wait_ge(s["add_done"], NU * g + u + 1)
                if c or u >= RING:
                    dve.wait_ge(s["y_done"], NU * g + u - RING + 1)
                dve.tensor_tensor_scan(h[:], a, pv[u % 2][:].rearrange("p n t -> p (n t)"), 0.0,
                                       ALU.mult, ALU.add).then_inc(s["scan_done"], 1)
                dve.wait_ge(s["scan_done"], NU * g + u + 1)
                h_end = h[:].rearrange("p (n t) -> p n t", n=N)[:, :, BT - 1]
                if b < NB - 1:
                    dve.tensor_tensor(first[:, et, :], a0[et][:, b + 1, :], h_end, ALU.mult
                                      ).then_inc(s["h_done"], 1)
                else:
                    dve.tensor_copy(hlast[:, et, :], h_end).then_inc(s["h_done"], 1)

            def skip_term(g, c, cc):
                q = c % 2
                dve.wait_ge(s["y_done"], NU * (g + 1))
                for e in range(ET):
                    dve.scalar_tensor_tensor(y[q][:, e, :], xc[q][:, e, :], prm[:, P_DP + e:P_DP + e + 1],
                                             y[q][:, e, :], ALU.mult, ALU.add).then_inc(s["ydp_done"], 1)

            def residual(g, c, cc):
                dve.wait_ge(s["out_done"], g + 1)
                dve.wait_ge(s["xo_loaded"], 16 * (g + 1))
                dve.tensor_tensor(xo[:], pC[:].rearrange("p (j d) -> p j d", j=TJ), xo[:], ALU.add
                                  ).then_inc(s["xo_done"], 1)

            def front(g, c, cc):
                x_norm(g, c, cc)
                conv(g, c, cc)
                step_size(g, c, cc)
                for b in range(NB):
                    moving(b)(g, c, cc)

            items = [(0, "front", x_norm),
                     (2, "back", skip_term),
                     (5, "front", conv), (7, "back", residual),
                     (9, "front", step_size),
                     (10, "front", moving(0)), (11, "front", moving(1)),
                     (11, "front", moving(2)), (12, "front", moving(3))]

            def main(g, c, cc):
                table = slots(items, g, c, cc)
                for u in range(NU):
                    for f in table.get(u, []):
                        f()
                    scan_unit(g, c, u)
                    if u >= 2:
                        sum_n(g, c, u - 2)
                    elif c:
                        sum_n(g - 1, c - 1, NU - 2 + u)

            def post(g, c, cc):
                sum_n(g, c, NU - 2)
                sum_n(g, c, NU - 1)
                skip_term(g, c, cc)
                residual(g, c, cc)

            layers(dve, prologue, front, main, post)

        @block.gpsimd
        def _(pool):
            def step_size(g, c, cc):
                q = c % 2
                pool.wait_ge(s["z_done"], g + 1)
                pool.tensor_tensor(dl[q][:], dl[q][:], t1, ALU.add).then_inc(s["sum_done"], 1)


            def times_c(g, c, u):
                _, b, _, _ = unit(u)
                h = ht[u % RING]
                pool.wait_ge(s["h_done"], NU * g + u + 1)
                if u < 2 * NB:
                    pool.wait_ge(cb_loaded[b], 16 * (g + 1))
                pool.tensor_tensor(h[:], h[:], cb[:, b, :], ALU.mult).then_inc(s["p_done"], 1)

            def gate(g, c, cc):
                q = c % 2
                pool.wait_ge(s["ydp_done"], ET * (g + 1))
                pool.wait_ge(s["proj_read"], PROJ * g + 4)
                pool.tensor_tensor(y[q][:], y[q][:], sz[q][:], ALU.mult).then_inc(s["gate_done"], 1)

            items = [(3, "back", gate), (8, "front", step_size)]

            def main(g, c, cc):
                table = slots(items, g, c, cc)
                for u in range(NU):
                    for f in table.get(u, []):
                        f()
                    times_c(g, c, u)

            layers(pool, lambda l: None, step_size, main, gate)



def build_experts(nc, ins, x0, x2, out):
    with ExitStack() as ctx:
        def sb(name, shape, dt=F32):
            return ctx.enter_context(nc.sbuf_tensor(name, shape, dt))

        def ps(name, shape, dt=F32):
            return ctx.enter_context(nc.psum_tensor(name, shape, dt))

        def sem(name):
            return ctx.enter_context(nc.semaphore("m_" + name))

        table = nc.dram_tensor("x1_table", [T, D], F32, kind="Internal").ap()
        total = nc.dram_tensor("x1_total", [T, D], F32, kind="Internal").ap()
        ET_ = NX * TT

        ident = sb("ident2", [P, P])
        upper = sb("upper", [P, P])
        ones = sb("ones", [P, P])
        iota = sb("iota", [P, P])
        place = sb("place", [P, TT, 2])
        w_ch = sb("w_ch", [P, DK, NX])
        eps2 = sb("eps2", [P, 1])
        xa = [sb(f"xa{q}", [P, GRP, D]) for q in range(2)]
        xb2 = [sb(f"xb2{q}", [P, GRP, D]) for q in range(2)]
        stats = sb("stats", [P, GRP, 6])
        mv_ = sb("mv_", [P, GRP, 2])
        rs = sb("rs", [P, GRP])
        xT = [sb(f"xT{i}", [P, 2, DK, P]) for i in range(2)]
        logit = sb("logit", [P, TT, NX])
        prob = sb("prob", [P, NX, TT])
        rowmax = sb("rowmax", [P, TT])
        rowsum = sb("rowsum", [P, TT])
        thr = sb("thr", [P, NX], U32)
        cand = sb("cand", [P, NX], U32)
        bit = sb("bit", [P, NX], U32)
        inc = sb("inc", [P, NX], U32)
        cnt = sb("cnt", [P, NX])
        need = sb("need", [P, NX])
        ge = sb("ge", [P, NX, TT])
        gt = sb("gt", [P, NX, TT])
        same = sb("same", [P, NX, TT])
        rank = sb("rank", [P, NX, TT])
        again = sb("again", [P, NX, TT])
        slot = sb("slot", [P, NX, TT], U32)
        slot_g = sb("slot_g", [P, NX, TT], U32)
        slot_p = sb("slot_p", [P, NX, TT], U32)
        hot_g = sb("hot_g", [P, ET_, CG], BF16)
        val = sb("val", [P, ET_, VALS], BF16)
        rest = sb("rest", [P, ET_])
        hot_val = sb("hot_val", [P, ET_, CG, VALS], BF16)
        hot_p = [sb(f"hot_p{i}", [P, TT, P], BF16) for i in range(2)]
        lists = sb("lists", [P, NX, CG, VALS])
        token = sb("token", [P, NX, CG], U32)
        gate = sb("gate", [P, NX, CG])
        token_e = [sb(f"token_e{q}", [P, CG], U32) for q in range(2)]
        gate_e = [sb(f"gate_e{q}", [P, CG]) for q in range(2)]
        w1 = [sb(f"w1{q}", [P, DK, F]) for q in range(2)]
        w2 = [sb(f"w2{q}", [P, FK, D]) for q in range(2)]
        xe = [xa[q] for q in range(2)]
        oe = [xb2[q] for q in range(2)]
        xeT = sb("xeT", [P, DK, CAP])
        hT = sb("hT", [P, FK, CAP])

        pX = [ps(f"pX{i}", [P, 2, DK, P]) for i in range(2)]
        pH = [ps(f"pH{i}", [P, 512]) for i in range(2)]
        pY = [ps(f"pY{i}", [P, 2, D]) for i in range(2)]
        pR = ps("pR", [P, 2, NX * TT])
        pN = ps("pN", [P, 512])

        names = ("const", "xin0", "xin1", "add", "stat", "aggr", "sqrt", "recip", "x1", "x1_kept", "xT_ps", "xT_sb",
                 "logit_ps", "logit_sb", "centred", "expd", "chain", "cnt", "tot", "eq", "ranked",
                 "sel", "placed", "hot", "listed", "weights0", "weights1", "chosen", "gathered0", "gathered1", "xeT_ps", "xeT_sb",
                 "h_ps", "h_sb", "y_ps", "gated", "added", "fin_in0", "fin_in1", "out", "eps", "waited_sp", "waited_pool")
        s = {n: sem(n) for n in names}
        block = ctx.enter_context(nc.Block())

        def rows(ap, k, tiles):
            return ap[bass.ds(k * (tiles * P), tiles * P), :].rearrange("(j p) d -> p j d", p=P)

        def pairs(eng, n, f):
            with eng.Fori(0, n // 2) as i:
                for q in range(2):
                    f(2 * i + q, q, i)

        @block.sync
        def _(sp):
            for t, n in ((ident, "ident"), (upper, "upper"), (ones, "ones"), (iota, "iota"),
                         (place, "place"), (w_ch, "w_ch"), (bit, "bit"), (again, "again")):
                sp.dma_start(t[:], ins[n]).then_inc(s["const"], 16)

            def load(k, q, i):
                sp.dma_start(xa[q][:], rows(x0, k, GRP)).then_inc(s[f"xin{q}"], 16)
                sp.dma_start(xb2[q][:], rows(x2, k, GRP)).then_inc(s[f"xin{q}"], 16)

            for q in range(2):
                load(q, q, 0)

            def keep(k):
                sp.wait_ge(s["x1"], k + 1)
                sp.dma_start(rows(table, k, GRP), xa[k % 2][:]).then_inc(s["x1_kept"], 16)
                sp.dma_start(rows(total, k, GRP), xa[k % 2][:]).then_inc(s["x1_kept"], 16)

            for k in range(NG):
                keep(k)
                if k + 2 < NG:
                    sp.wait_ge(s["x1_kept"], 32 * (k + 1))
                    sp.wait_ge(s["xT_ps"], GRP // 2 * (k + 1))
                    load(k + 2, k % 2, 0)

            for q in range(2):
                sp.dma_start(w1[q][:], ins["w1"][q]).then_inc(s[f"weights{q}"], 16)
                sp.dma_start(w2[q][:], ins["w2"][q]).then_inc(s[f"weights{q}"], 16)
            with sp.Fori(1, NX // 2) as i:
                for q in range(2):
                    sp.wait_ge(s["y_ps"], CG // 2 * (2 * i + q - 1))
                    take_waits(sp, s["waited_sp"])
                    e = 2 * i + q
                    sp.dma_start(w1[q][:], ins["w1"][bass.ds(e, 1)].rearrange("a p k n -> p (a k) n")
                                 ).then_inc(s[f"weights{q}"], 16)
                    sp.dma_start(w2[q][:], ins["w2"][bass.ds(e, 1)].rearrange("a p k n -> p (a k) n")
                                 ).then_inc(s[f"weights{q}"], 16)

            sp.wait_ge(s["added"], 16 * CG * NX)
            for q in range(2):
                sp.dma_start(xa[q][:], rows(total, q, GRP)).then_inc(s[f"fin_in{q}"], 16)
            for k in range(NG):
                sp.wait_ge(s["x1"], NG + k + 1)
                sp.dma_start(rows(out, k, GRP), xa[k % 2][:]).then_inc(s["out"], 16)
                if k + 2 < NG:
                    sp.wait_ge(s["out"], 16 * (k + 1))
                    sp.dma_start(xa[k % 2][:], rows(total, k + 2, GRP)).then_inc(s[f"fin_in{k % 2}"], 16)
            sp.wait_ge(s["out"], 16 * NG)

        @block.scalar
        def _(act):
            act.wait_ge(s["eps"], 1)

            def std(k):
                act.wait_ge(s["aggr"], GRP * (k + 1))
                if k:
                    act.wait_ge(s["x1"], k)
                act.activation(rs[:], mv_[:, :, 1], ACT.Sqrt, bias=eps2[:, 0:1]).then_inc(s["sqrt"], 1)

            for k in range(NG):
                std(k)
                for i in range(GRP // 2):
                    n = k * (GRP // 2) + i
                    act.wait_ge(s["xT_ps"], n + 1)
                    if n >= 2:
                        act.wait_ge(s["logit_ps"], 2 * (n - 1))
                    act.activation(xT[n % 2][:], pX[n % 2][:], ACT.Copy).then_inc(s["xT_sb"], 1)
                act.wait_ge(s["logit_ps"], GRP * (k + 1))
                act.activation(logit[:, k * GRP:(k + 1) * GRP, :],
                               pN[:, 0:GRP * NX].rearrange("p (j e) -> p j e", e=NX), ACT.Copy
                               ).then_inc(s["logit_sb"], 1)
            act.wait_ge(s["centred"], 1)
            act.activation(logit[:], logit[:], ACT.Exp).then_inc(s["expd"], 1)

            def expert(e, q, i):
                for j in range(CG // 2):
                    n = e * (CG // 2) + j
                    act.wait_ge(s["xeT_ps"], n + 1)
                    if j == 0:
                        act.wait_ge(s["h_ps"], e * (2 * FK))
                    act.activation(xeT[:, :, 2 * j * P:(2 * j + 2) * P],
                                   pX[j % 2][:].rearrange("p a k c -> p (a k c)").rearrange(
                                       "p (k c) -> p k c", k=DK), ACT.Copy).then_inc(s["xeT_sb"], 1)
                for h in range(2):
                    for f in range(FK):
                        m = h * FK + f
                        act.wait_ge(s["h_ps"], e * (2 * FK) + m + 1)
                        if m == 0:
                            act.wait_ge(s["y_ps"], e * (CG // 2))
                        act.activation(hT[:, f, h * 512:(h + 1) * 512], pH[m % 2][:], ACT.Silu
                                       ).then_inc(s["h_sb"], 1)

            pairs(act, NX, expert)
            for k in range(NG):
                std(NG + k)

        @block.tensor
        def _(pe):
            pe.wait_ge(s["const"], 16 * 8)
            for k in range(NG):
                pe.wait_ge(s["x1"], k + 1)

                def logits(n):
                    pe.wait_ge(s["xT_sb"], n + 1)
                    if n % (GRP // 2) == 0 and n:
                        pe.wait_ge(s["logit_sb"], n // (GRP // 2))
                    for a in range(2):
                        t = (2 * n + a) % GRP
                        for c in range(DK):
                            mm = pe.matmul(pN[:, t * NX:(t + 1) * NX], xT[n % 2][:, a, c, :], w_ch[:, c, :],
                                           start=(c == 0), stop=(c == DK - 1))
                        mm.then_inc(s["logit_ps"], 1)

                for i in range(GRP // 2):
                    n = k * (GRP // 2) + i
                    if n >= 2:
                        pe.wait_ge(s["xT_sb"], n - 1)
                    for a in range(2):
                        for c in range(DK):
                            mm = pe.transpose(pX[n % 2][:, a, c, :], xa[k % 2][:, 2 * i + a, c * P:(c + 1) * P],
                                              ident[:])
                    mm.then_inc(s["xT_ps"], 1)
                    if i:
                        logits(n - 1)
                logits(k * (GRP // 2) + GRP // 2 - 1)
            pe.wait_ge(s["logit_sb"], NG)
            with pe.Fori(0, BITS) as i:
                pe.wait_ge(s["cnt"], i + 1)
                pe.matmul(pN[:, 0:NX], ones[:], cnt[:], start=True, stop=True).then_inc(s["tot"], 1)
            pe.wait_ge(s["cnt"], BITS + 1)
            pe.matmul(pN[:, 0:NX], ones[:], cnt[:], start=True, stop=True).then_inc(s["tot"], 1)
            for n in range(2):
                src = (same, gt)[n]
                pe.wait_ge(s["eq"], n + 1)
                flat = src[:].rearrange("p e t -> p (e t)")
                pe.matmul(pR[:, 0, :], upper[:], flat, start=True, stop=True)
                pe.matmul(pR[:, 1, :], ones[:], flat, start=True, stop=True).then_inc(s["ranked"], 1)
            for e in range(NX):
                pe.wait_ge(s["hot"], e + 1)
                for t in range(TT):
                    mm = pe.matmul(pH[0][:, e * CG * VALS:(e + 1) * CG * VALS], hot_p[e % 2][:, t, :],
                                   hot_val[:, e * TT + t, :, :].rearrange("p g v -> p (g v)"),
                                   start=(t == 0), stop=(t == TT - 1))
                mm.then_inc(s["listed"], 1)

            def expert(e, q, i):
                for j in range(CG // 2):
                    if j == 0:
                        pe.wait_ge(s[f"gathered{q}"], i * (16 * CG) + 16 * CG)
                        pe.wait_ge(s[f"weights{q}"], i * 32 + 32)
                        pe.wait_ge(s["xeT_sb"], e * (CG // 2))
                    elif j >= 2:
                        pe.wait_ge(s["xeT_sb"], e * (CG // 2) + j - 1)
                    for c in range(DK):
                        for a in range(2):
                            flat = pX[j % 2][:].rearrange("p a k c -> p (a k c)")
                            mm = pe.transpose(flat[:, (2 * c + a) * P:(2 * c + a + 1) * P],
                                              xe[q][:, 2 * j + a, c * P:(c + 1) * P], ident[:])
                    mm.then_inc(s["xeT_ps"], 1)
                for h in range(2):
                    pe.wait_ge(s["xeT_sb"], e * (CG // 2) + 2 * (h + 1))
                    for f in range(FK):
                        m = h * FK + f
                        pe.wait_ge(s["h_sb"], e * (2 * FK) + m - 1) if m >= 2 else pe.wait_ge(
                            s["h_sb"], e * (2 * FK))
                        for c in range(DK):
                            mm = pe.matmul(pH[m % 2][:], w1[q][:, c, f * P:(f + 1) * P],
                                           xeT[:, c, h * 512:(h + 1) * 512],
                                           start=(c == 0), stop=(c == DK - 1))
                        mm.then_inc(s["h_ps"], 1)
                for j in range(CG // 2):
                    if j == 0 or j == 2:
                        pe.wait_ge(s["h_sb"], e * (2 * FK) + FK * (j // 2 + 1))
                    if j >= 2:
                        pe.wait_ge(s["gated"], e * CG + 2 * (j - 1))
                    else:
                        pe.wait_ge(s["gated"], e * CG)
                    for a in range(2):
                        g = 2 * j + a
                        for f in range(FK):
                            mm = pe.matmul(pY[j % 2][:, a, :], hT[:, f, g * P:(g + 1) * P], w2[q][:, f, :],
                                           start=(f == 0), stop=(f == FK - 1))
                    mm.then_inc(s["y_ps"], 1)

            pe.wait_ge(s["chosen"], 1)
            pairs(pe, NX, expert)

        @block.vector
        def _(dve):
            dve.memset(eps2[:], EPS).then_inc(s["eps"], 1)

            count = [0]

            def link(i):
                count[0] += 1
                i.then_inc(s["chain"], 1)
                dve.wait_ge(s["chain"], count[0])

            def normalise(k, q):
                if k:
                    dve.wait_ge(s["sqrt"], k)
                for j in range(GRP):
                    dve.bn_stats(stats[:, j, :], xa[q][:, j, :]).then_inc(s["stat"], 1)
                for j in range(GRP):
                    dve.wait_ge(s["stat"], GRP * k + j + 1)
                    dve.bn_aggr(mv_[:, j, :], stats[:, j, :]).then_inc(s["aggr"], 1)
                dve.wait_ge(s["sqrt"], k + 1)
                dve.reciprocal(rs[:], rs[:]).then_inc(s["recip"], 1)
                dve.wait_ge(s["recip"], k + 1)
                for j in range(GRP):
                    i = dve.tensor_scalar(xa[q][:, j, :], xa[q][:, j, :], mv_[:, j, 0:1], rs[:, j:j + 1],
                                          ALU.subtract, ALU.mult)
                i.then_inc(s["x1"], 1)
                dve.wait_ge(s["x1"], k + 1)

            for k in range(NG):
                q = k % 2
                dve.wait_ge(s[f"xin{q}"], 32 * (k // 2 + 1))
                dve.tensor_tensor(xa[q][:], xa[q][:], xb2[q][:], ALU.add).then_inc(s["add"], 1)
                dve.wait_ge(s["add"], k + 1)
                normalise(k, q)

            def over_e(v):
                return v.rearrange("p (t o) -> p t o", o=1).broadcast_to([P, TT, NX])

            dve.wait_ge(s["logit_sb"], NG)
            link(dve.tensor_reduce(rowmax[:], logit[:], AXX, ALU.max))
            dve.tensor_tensor(logit[:], logit[:], over_e(rowmax[:]), ALU.subtract).then_inc(s["centred"], 1)
            dve.wait_ge(s["expd"], 1)
            link(dve.tensor_reduce(rowsum[:], logit[:], AXX, ALU.add))
            link(dve.reciprocal(rowsum[:], rowsum[:]))
            link(dve.tensor_tensor(prob[:].rearrange("p e t -> p t e"), logit[:], over_e(rowsum[:]), ALU.mult))

            def per_e(v):
                return v.rearrange("p (e o) -> p e o", o=1).broadcast_to([P, NX, TT])

            dve.wait_ge(s["const"], 16 * 8)
            link(dve.memset(thr[:], 0))
            base, steps = count[0], 5
            with dve.Fori(0, BITS) as i:
                def step(k, ins_):
                    ins_.then_inc(s["chain"], 1)
                    dve.wait_ge(s["chain"], i * steps + (base + k))

                step(1, dve.tensor_tensor(cand[:], thr[:], bit[:], ALU.bitwise_or))
                step(2, dve.tensor_tensor(ge[:], prob[:], per_e(cand[:].bitcast(F32)), ALU.is_ge))
                dve.tensor_reduce(cnt[:], ge[:], AXX, ALU.add).then_inc(s["cnt"], 1)
                dve.wait_ge(s["tot"], i + 1)
                step(3, dve.scalar_tensor_tensor(inc[:], pN[:, 0:NX], CAP - 0.5, bit[:], ALU.is_ge, ALU.mult))
                step(4, dve.tensor_tensor(thr[:], thr[:], inc[:], ALU.bitwise_or))
                step(5, dve.tensor_single_scalar(bit[:], bit[:], 1, ALU.logical_shift_right))
            count[0] = base + steps * BITS

            dve.tensor_tensor(same[:], prob[:], per_e(thr[:].bitcast(F32)), ALU.is_equal).then_inc(s["eq"], 1)
            link(dve.tensor_tensor(gt[:], prob[:], per_e(thr[:].bitcast(F32)), ALU.is_gt))
            dve.tensor_reduce(cnt[:], gt[:], AXX, ALU.add).then_inc(s["cnt"], 1)
            dve.wait_ge(s["tot"], BITS + 1)
            link(dve.tensor_scalar(need[:], pN[:, 0:NX], -1.0, float(CAP), ALU.mult, ALU.add))

            def ranks(n):
                flat = rank[:].rearrange("p e t -> p (e t)")
                dve.wait_ge(s["ranked"], n + 1)
                link(dve.tensor_tensor_scan(flat, again[:].rearrange("p e t -> p (e t)"), pR[:, 1, :],
                                            0.0, ALU.mult, ALU.add))
                link(dve.tensor_tensor(flat, flat, pR[:, 1, :], ALU.subtract))
                link(dve.tensor_tensor(flat, flat, pR[:, 0, :], ALU.add))

            ranks(0)
            link(dve.tensor_tensor(ge[:], rank[:], per_e(need[:]), ALU.is_le))
            link(dve.tensor_tensor(ge[:], ge[:], same[:], ALU.mult))
            dve.tensor_tensor(gt[:], gt[:], ge[:], ALU.add).then_inc(s["eq"], 1)
            dve.wait_ge(s["eq"], 2)
            ranks(1)
            FAR = 8 * CAP
            link(dve.scalar_tensor_tensor(rank[:], rank[:], float(-1 - FAR), gt[:], ALU.add, ALU.mult))
            link(dve.tensor_scalar(slot[:], rank[:], float(FAR), None, ALU.add))
            dve.tensor_single_scalar(slot_g[:], slot[:], 7, ALU.logical_shift_right)
            link(dve.tensor_single_scalar(slot_p[:], slot[:], P - 1, ALU.bitwise_and))
            sg = slot_g[:].rearrange("p e (t o) -> p (e t) o", o=1).broadcast_to([P, ET_, CG])
            dve.tensor_tensor(hot_g[:], iota[:, 0:CG].rearrange("p (o g) -> p o g", o=1)
                              .broadcast_to([P, ET_, CG]), sg, ALU.is_equal)
            for e in range(NX):
                dve.tensor_copy(val[:, e * TT:(e + 1) * TT, 0:2], place[:])
            pf = prob[:].rearrange("p e t -> p (e t)")
            link(dve.tensor_copy(val[:, :, 2], pf))
            link(dve.tensor_tensor(rest[:], pf, val[:, :, 2], ALU.subtract))
            link(dve.tensor_copy(val[:, :, 3], rest[:]))
            link(dve.tensor_tensor(rest[:], rest[:], val[:, :, 3], ALU.subtract))
            link(dve.tensor_copy(val[:, :, 4], rest[:]))
            link(dve.tensor_tensor(
                hot_val[:], hot_g[:].rearrange("p c (g o) -> p c g o", o=1).broadcast_to([P, ET_, CG, VALS]),
                val[:].rearrange("p c (o v) -> p c o v", o=1).broadcast_to([P, ET_, CG, VALS]), ALU.mult))
            for e in range(NX):
                if e >= 2:
                    dve.wait_ge(s["listed"], e - 1)
                dve.tensor_tensor(hot_p[e % 2][:], iota[:].rearrange("p (o c) -> p o c", o=1)
                                  .broadcast_to([P, TT, P]),
                                  slot_p[:, e, :].rearrange("p (t o) -> p t o", o=1)
                                  .broadcast_to([P, TT, P]), ALU.is_equal).then_inc(s["hot"], 1)
            dve.wait_ge(s["listed"], NX)
            link(dve.tensor_copy(lists[:].rearrange("p e g v -> p (e g v)"), pH[0][:, 0:NX * CG * VALS]))
            link(dve.scalar_tensor_tensor(token[:], lists[:, :, :, 0], float(P), lists[:, :, :, 1],
                                          ALU.mult, ALU.add))
            link(dve.tensor_tensor(gate[:], lists[:, :, :, 2], lists[:, :, :, 3], ALU.add))
            dve.tensor_tensor(gate[:], gate[:], lists[:, :, :, 4], ALU.add).then_inc(s["chosen"], 1)
            dve.wait_ge(s["chosen"], 1)

            def choose(e, q):
                dve.tensor_copy(gate_e[q][:], gate[:, bass.ds(e, 1), :].rearrange("p a g -> p (a g)"))
                dve.tensor_copy(token_e[q][:], token[:, bass.ds(e, 1), :].rearrange("p a g -> p (a g)")
                                ).then_inc(s["chosen"], 1)

            choose(0, 0)

            def expert(e, q, i):
                dve.wait_ge(s["added"], e * (16 * CG))
                if q == 0:
                    choose(e + 1, 1)
                else:
                    dve.tensor_copy(gate_e[0][:], gate[:, bass.ds(nxt(i), 1), :].rearrange("p a g -> p (a g)"))
                    dve.tensor_copy(token_e[0][:], token[:, bass.ds(nxt(i), 1), :].rearrange(
                        "p a g -> p (a g)")).then_inc(s["chosen"], 1)
                for j in range(CG // 2):
                    dve.wait_ge(s["y_ps"], e * (CG // 2) + j + 1)
                    for a in range(2):
                        g = 2 * j + a
                        dve.tensor_scalar(oe[q][:, g, :], pY[j % 2][:, a, :], gate_e[q][:, g:g + 1], None,
                                          ALU.mult).then_inc(s["gated"], 1)

            def nxt(i):
                return i * 2 + 2

            with dve.Fori(0, NX // 2 - 1) as i:
                for q in range(2):
                    expert(2 * i + q, q, i)
            last = NX // 2 - 1
            expert(2 * last, 0, last)
            e = NX - 1
            for j in range(CG // 2):
                dve.wait_ge(s["y_ps"], e * (CG // 2) + j + 1)
                for a in range(2):
                    g = 2 * j + a
                    dve.tensor_scalar(oe[1][:, g, :], pY[j % 2][:, a, :], gate_e[1][:, g:g + 1], None,
                                      ALU.mult).then_inc(s["gated"], 1)

            for k in range(NG):
                dve.wait_ge(s[f"fin_in{k % 2}"], 16 * (k // 2 + 1))
                normalise(NG + k, k % 2)

        @block.gpsimd
        def _(pool):
            pool.wait_ge(s["x1_kept"], 32 * NG)

            def gather(e, q):
                pool.wait_ge(s["chosen"], e + 2)
                pool.wait_ge(s["xeT_ps"], (e - 1) * (CG // 2))
                take_waits(pool, s["waited_pool"])
                for g in range(CG):
                    pool.indirect_dma_start(xe[q][:, g, :], None, table, bass.IndirectOffsetOnAxis(
                        ap=token_e[q][:, g:g + 1], axis=0)).then_inc(s[f"gathered{q}"], 16)

            def scatter(e, q):
                pool.wait_ge(s["added"], e * (16 * CG))
                for g in range(CG):
                    pool.wait_ge(s["gated"], e * CG + g + 1)
                    take_waits(pool, s["waited_pool"])
                    pool.indirect_dma_start(total, bass.IndirectOffsetOnAxis(
                        ap=token_e[q][:, g:g + 1], axis=0), oe[q][:, g, :], None,
                        compute_op=ALU.add).then_inc(s["added"], 16)

            pool.wait_ge(s["chosen"], 2)
            for g in range(CG):
                pool.indirect_dma_start(xe[0][:, g, :], None, table, bass.IndirectOffsetOnAxis(
                    ap=token_e[0][:, g:g + 1], axis=0)).then_inc(s["gathered0"], 16)
            with pool.Fori(0, NX // 2 - 1) as i:
                for q in range(2):
                    e = 2 * i + q
                    gather(e + 1, 1 - q)
                    scatter(e, q)
            gather(NX - 1, 1)
            scatter(NX - 2, 0)
            scatter(NX - 1, 1)



def kernel(**inputs):
    import numpy as np
    import concourse.bacc as bacc
    from concourse.bass_utils import run_bass_kernel_spmd

    a = {k: np.asarray(v) for k, v in inputs.items()}

    def tiles(w):
        return w.reshape(w.shape[0], -1, P, w.shape[2]).transpose(0, 2, 1, 3)

    x_proj = a["L0_attn_x_proj_w"].transpose(0, 2, 1)
    w_xp = np.zeros((NL, E, DBC), np.float32)
    for to, part in ((0, 0), (B_ROW, R), (C_ROW, R + N)):
        w_xp[:, :, to:to + N] = x_proj[:, :, part:part + N]
    per_channel = [a["L0_attn_norm_w"].reshape(NL, DK, P).transpose(0, 2, 1),
                   a["L0_attn_conv_w"].reshape(NL, ET, P, TAPS).transpose(0, 2, 1, 3).reshape(NL, P, -1)]
    per_channel += [a[k].reshape(NL, ET, P).transpose(0, 2, 1)
                    for k in ("L0_attn_conv_b", "L0_attn_dt_b", "L0_attn_Dp")]
    steps = np.arange(BT)
    lag = steps[None, :] - steps[:, None]
    carry = np.zeros((N, N, BT), np.float32)
    carry[np.arange(N), np.arange(N), :] = BETA ** (steps + 1.0)
    again = np.ones((P, NX, TT), np.float32)
    again[:, :, 0] = 0.0
    place = np.empty((P, TT, 2), np.float32)
    place[:, :, 0] = np.arange(TT)[None, :]
    place[:, :, 1] = np.arange(P)[:, None]
    arrays = {
        "x": a["L0_attn_x"][0],
        "w_in": tiles(a["L0_attn_in_proj_w"].transpose(0, 2, 1)),
        "w_out": tiles(a["L0_attn_out_w"].transpose(0, 2, 1)),
        "w_xp": tiles(w_xp),
        "w_dt": a["L0_attn_dt_w"].transpose(0, 2, 1),
        "prm": np.concatenate(per_channel, axis=2),
        "a_log": a["L0_attn_A_log"].reshape(NL, ET, P, N).transpose(0, 2, 1, 3),
        "ident": np.eye(P, dtype=np.float32),
        "tri": np.where(lag >= 0, -BETA ** np.maximum(lag, 0).astype(np.float64), 0.0).astype(np.float32),
        "carry": carry,
        "upper": np.triu(np.ones((P, P), np.float32)),
        "ones": np.ones((P, P), np.float32),
        "iota": np.broadcast_to(np.arange(P, dtype=np.float32), (P, P)),
        "place": place,
        "bit": np.full((P, NX), 1 << (BITS - 1), np.uint32),
        "again": again,
        "w_ch": a["L0_ffn_choice_w"].T.reshape(DK, P, NX).transpose(1, 0, 2),
        "w1": tiles(a["L0_ffn_w1"]),
        "w2": tiles(a["L0_ffn_w2"]),
    }
    arrays = {k: np.ascontiguousarray(v) for k, v in arrays.items()}
    nc = bacc.Bacc("TRN2", target_bir_lowering=False, num_devices=1)
    ins = {}
    for k, v in arrays.items():
        ins[k] = nc.dram_tensor("in_" + k, v.shape, mybir.dt.from_np(v.dtype), kind="ExternalInput").ap()
    out = nc.dram_tensor("out", [T, D], F32, kind="ExternalOutput").ap()
    seq = nc.dram_tensor("seq", [(NL + 1) * T, D], F32, kind="Internal").ap()
    build_mamba(nc, ins, seq)
    build_experts(nc, ins, ins["x"], seq[NL * T:(NL + 1) * T, :], out)
    r = run_bass_kernel_spmd(nc, [{"in_" + k: v for k, v in arrays.items()}], core_ids=[0])
    return r.results[0]["out"].reshape(1, T, D)
```

```python
from contextlib import ExitStack

import concourse.bass as bass
from concourse import mybir

F32 = mybir.dt.float32
BF16 = mybir.dt.bfloat16
U32 = mybir.dt.uint32
ALU = mybir.AluOpType
ACT = mybir.ActivationFunctionType
AXX = mybir.AxisListType.X

P = 128
T = 4096
D = 256
DK = D // P
E = 512
ET = E // P
N = 16
R = 16
TAPS = 4
BETA = 0.6
EPS = 1e-5
NL = 2
TC = 256
NC = T // TC
BT = 64
NB = TC // BT
TJ = TC // P
KV = BT + 64
HN = 8
NU = ET * NB
DBC = 96
B_ROW, C_ROW = 32, 64
U_FLOOR = 2.0 ** -80
PROJ = 7
RING = 4

P_NORM = 0
P_CW = P_NORM + DK
P_CB = P_CW + ET * TAPS
P_DTB = P_CB + ET
P_DP = P_DTB + ET
P_ALL = P_DP + ET

NX = 8
CAP = T * 2 // NX
F = 512
FK = F // P
TT = T // P
CG = CAP // P
GRP = 8
NG = TT // GRP
VALS = 5
EXP_LN_SET = 6
BITS = 30
ROUNDS = BITS // 2
DIG = 3


def take_waits(eng, waited):
    eng.sem_inc(waited, 1)


def load_exp_ln(nc, act):
    act.add_instruction(mybir.InstLoadActFuncSet(
        name=nc.get_next_instruction_name(), engine=mybir.EngineType.Activation, act_func_set_id=EXP_LN_SET))


def unit(u):
    pair, rest = divmod(u, 2 * NB)
    b, e = divmod(rest, 2)
    return pair, b, e, 2 * pair + e


def build_mamba(nc, ins, seq):
    with ExitStack() as ctx:
        def sb(name, shape, dt=F32):
            return ctx.enter_context(nc.sbuf_tensor(name, shape, dt))

        def ps(name, shape, dt=F32):
            return ctx.enter_context(nc.psum_tensor(name, shape, dt))

        def sem(name):
            return ctx.enter_context(nc.semaphore(name))

        c_dram = nc.dram_tensor("c_rows", [2, NB, N, BT], F32, kind="Internal").ap()

        w_in = sb("w_in", [P, DK, 2 * E])
        w_out = sb("w_out", [P, ET, D])
        w_xp = sb("w_xp", [P, ET, DBC])
        w_dt = sb("w_dt", [DBC, E])
        prm = sb("prm", [P, P_ALL])
        rate = sb("rate", [P, ET, N])
        ident = sb("ident", [P, P])
        tri = sb("tri", [BT, BT])
        zcol = sb("zcol", [P, NB * N])
        ssq = sb("ssq", [P, TT])
        rstd = sb("rstd", [P, TT])
        x_in = sb("x_in", [P, TJ, D])
        xnT = x_in[:].rearrange("p j d -> p (j d)").rearrange("p (k t) -> p k t", k=DK)
        tmp1 = sb("tmp1", [P, ET * TC])
        t1 = tmp1[:, :].rearrange("p (e t) -> p e t", e=ET)
        tmp3 = sb("tmp3", [P, ET * (TC + TAPS - 1)])
        xb = tmp3[:, :].rearrange("p (e t) -> p e t", e=ET)
        t3 = tmp3[:, 0:ET * TC].rearrange("p (e t) -> p e t", e=ET)
        eps_col = sb("eps_col", [P, 1])
        one_col = sb("one_col", [P, 1])
        halo = sb("halo", [P, ET, TAPS - 1])
        xc = [sb(f"xc{q}", [P, ET, TC]) for q in range(2)]
        sz = [sb(f"sz{q}", [P, ET, TC]) for q in range(2)]
        dl = [sb(f"dl{q}", [P, ET, TC]) for q in range(2)]
        dbc = sb("dbc", [DBC, TC])
        mv = [[sb(f"mv{q}{b}", [KV, N, BT]) for b in range(NB)] for q in range(2)]
        ut = [[sb(f"ut{q}{b}", [KV, E]) for b in range(NB)] for q in range(2)]
        da = [sb(f"da{e}", [P, NB, N, BT]) for e in range(ET)]
        a0 = [sb(f"a0{e}", [P, NB, N]) for e in range(ET)]
        cb = sb("cb", [P, NB, N * BT])
        ht = [sb(f"ht{r}", [P, N * BT]) for r in range(RING)]
        first = sb("first", [P, ET, N])
        hlast = sb("hlast", [P, ET, N])
        y = [sb(f"y{q}", [P, ET, TC]) for q in range(2)]
        xo = sb("xo", [P, TJ, D])

        x_all = [da[e][:].rearrange("p b n t -> p (b n t)").rearrange("p (j d) -> p j d", d=D)
                 for e in range(2)]

        pv = [ps(f"pv{s}", [P, N, BT]) for s in range(2)]
        pp = [ps(f"pp{s}", [P, 2, TC]) for s in range(2)]
        pT = ps("pT", [P, 512])
        pC = ps("pC", [P, 512])

        s = {n: sem("s_" + n) for n in (
            "x_copied", "const_loaded", "x0_loaded0", "x0_loaded1", "squared", "ssq_done",
            "w_loaded", "sqrt_done", "rstd_done", "rate", "zeroed", "x_loaded", "xn_done",
            "xT_done", "xnT_done", "halo_done", "proj_done", "proj_read", "tap0_done", "tap_done",
            "xc_done", "exp_neg_done", "one_plus_done", "correction_done", "ln_done", "sum_done",
            "dl_done", "u_done", "bT_done", "moving_done", "uT_done", "ut_done", "carry_done",
            "carry_read", "c_stored", "exp_done", "a0_copied", "a_done", "v_done", "first_done",
            "add_done", "scan_done", "h_done", "p_done", "y_done", "ydp_done", "gate_done",
            "out_done", "xo_loaded", "xo_done", "xo_stored", "sq_done", "halo_set", "padded",
            "rest_copied", "waited_sp", "waited_pe")}
        cb_loaded = [sem(f"cb_loaded{b}") for b in range(NB)]

        block = ctx.enter_context(nc.Block())

        def layers(eng, prologue, front, main, post):
            with eng.Fori(0, NL) as l:
                prologue(l)
                front(l * NC, 0, 0)
                main(l * NC, 0, 0)
                with eng.Fori(0, (NC - 2) // 2) as i:
                    for j in range(2):
                        main(l * NC + 2 * i + 1 + j, 1 + j, 2 * i + 1 + j)
                main(l * NC + NC - 1, NC - 1, NC - 1)
                post(l * NC + NC - 1, NC - 1, NC - 1)

        def slots(items, g, c, cc):
            table = {}
            for slot, kind, f in items:
                if kind == "front" and c != NC - 1:
                    table.setdefault(slot, []).append(lambda f=f: f(g + 1, c + 1, cc + 1))
                if kind == "back" and c != 0:
                    table.setdefault(slot, []).append(lambda f=f: f(g - 1, c - 1, cc - 1))
            return table

        @block.sync
        def _(sp):
            sp.dma_start(ident[:], ins["ident"]).then_inc(s["const_loaded"], 16)
            sp.dma_start(tri[:], ins["tri"]).then_inc(s["const_loaded"], 16)
            for q in range(2):
                for b in range(NB):
                    sp.dma_start(mv[q][b][BT:KV, :, :], ins["carry"]).then_inc(s["const_loaded"], 16)
            sp.wait_ge(s["x0_loaded1"], 16)
            sp.dma_start(seq[0:2 * TC, :], ins["x"][0:2 * TC, :]).then_inc(s["x_copied"], 16)
            sp.wait_ge(s["x_copied"], 16)

            def load_x(g, c, cc):
                if c:
                    sp.wait_ge(s["proj_done"], PROJ * (g - 1) + 4)
                    take_waits(sp, s["waited_sp"])
                sp.dma_start(x_in[:], seq[bass.ds(g * TC, TC), :].rearrange(
                    "(j p) d -> p j d", p=P)).then_inc(s["x_loaded"], 16)

            def load_c(g, c, cc):
                q = c % 2
                sp.wait_ge(s["proj_read"], PROJ * g + 5)
                take_waits(sp, s["waited_sp"])
                sp.dma_start(c_dram[q].rearrange("b n t -> n b t"),
                             dbc[C_ROW:C_ROW + N, :].rearrange("n (b t) -> n b t", b=NB)
                             ).then_inc(s["c_stored"], 16)
                sp.wait_ge(s["c_stored"], 16 * g + 16)
                take_waits(sp, s["waited_sp"])
                for b in range(NB):
                    if c:
                        sp.wait_ge(s["p_done"], NU * (g - 1) + 2 * NB + 2 * b + 2)
                        take_waits(sp, s["waited_sp"])
                    sp.dma_start(cb[:, b, :], c_dram[q, b].rearrange("n t -> (n t)")
                                 .partition_broadcast(P)).then_inc(cb_loaded[b], 16)

            def load_xo(g, c, cc):
                if c:
                    sp.wait_ge(s["xo_stored"], 16 * g)
                    take_waits(sp, s["waited_sp"])
                    sp.wait_ge(s["sq_done"], g)
                    take_waits(sp, s["waited_sp"])
                sp.dma_start(xo[:], seq[bass.ds(g * TC, TC), :].rearrange(
                    "(j p) d -> p j d", p=P)).then_inc(s["xo_loaded"], 16)

            def store_xo(g, c, cc):
                sp.wait_ge(s["xo_done"], g + 1)
                take_waits(sp, s["waited_sp"])
                sp.dma_start(seq[bass.ds((g + NC) * TC, TC), :].rearrange(
                    "(j p) d -> p j d", p=P), xo[:]).then_inc(s["xo_stored"], 16)

            def prologue(l):
                sp.wait_ge(s["xo_stored"], l * (16 * NC))
                take_waits(sp, s["waited_sp"])
                sp.wait_ge(s["sq_done"], l * NC)
                take_waits(sp, s["waited_sp"])
                one = bass.ds(l, 1)
                for dst, name in ((w_in, "w_in"), (w_out, "w_out"), (w_xp, "w_xp")):
                    sp.dma_start(dst[:], ins[name][one].rearrange("a p k n -> p (a k) n")
                                 ).then_inc(s["w_loaded"], 16)
                sp.dma_start(w_dt[:], ins["w_dt"][one].rearrange("a r n -> r (a n)")
                             ).then_inc(s["w_loaded"], 16)
                sp.dma_start(prm[:], ins["prm"][one].rearrange("a p n -> p (a n)")
                             ).then_inc(s["w_loaded"], 16)
                sp.dma_start(rate[:], ins["a_log"][one].rearrange("a p e n -> p (a e) n")
                             ).then_inc(s["w_loaded"], 16)

            def main(g, c, cc):
                if c:
                    load_xo(g - 1, c - 1, None)
                if c < NC - 2:
                    load_x(g + 2, c + 2, None)
                if c:
                    store_xo(g - 1, c - 1, None)
                if c < NC - 1:
                    load_c(g + 1, c + 1, None)

            with sp.Fori(0, NL) as l:
                g0 = l * NC
                prologue(l)
                load_x(g0, 0, 0)
                load_x(g0 + 1, 1, 1)
                sp.wait_ge(s["rest_copied"], 16)
                load_c(g0, 0, 0)
                main(g0, 0, 0)
                with sp.Fori(0, (NC - 4) // 2) as i:
                    for j in range(2):
                        main(g0 + 2 * i + 1 + j, 1 + j, None)
                for c in range(NC - 3, NC):
                    main(g0 + c, c, c)
                load_xo(g0 + NC - 1, NC - 1, NC - 1)
                store_xo(g0 + NC - 1, NC - 1, NC - 1)
            sp.wait_ge(s["xo_stored"], 16 * NC * NL)

        W_ALL = 16 * 6

        @block.scalar
        def _(act):
            for h in range(2):
                act.dma_start(x_all[h], ins["x"][bass.ds(h * (T // 2), T // 2), :].rearrange(
                    "(j p) d -> p j d", p=P)).then_inc(s[f"x0_loaded{h}"], 16)
            act.wait_ge(s["x0_loaded0"], 16)
            for j in range(TT // 2):
                act.activation(x_all[0][:, j, :], x_all[0][:, j, :], ACT.Square,
                               accum_out=ssq[:, j:j + 1]).then_inc(s["ssq_done"], 1)

            def prologue(l):
                act.wait_ge(s["padded"], 2 * NB)
                act.wait_ge(s["ssq_done"], TT // 2 + 1)
                act.wait_ge(s["sq_done"], l * NC)
                act.wait_ge(s["zeroed"], 1)
                act.activation(rstd[:], ssq[:], ACT.Sqrt, scale=1.0 / D, bias=eps_col[:, 0:1]
                               ).then_inc(s["sqrt_done"], 1)
                act.wait_ge(s["w_loaded"], W_ALL * (l + 1))
                act.activation(rate[:], rate[:], ACT.Exp).then_inc(s["rate"], 1)
                act.wait_ge(s["rate"], l + 1)

            def halo_front(g, c, cc):
                if c == 0:
                    act.wait_ge(s["zeroed"], 1)
                    act.activation(xb[:, :, 0:TAPS - 1], zcol[:, 0:ET * (TAPS - 1)].rearrange(
                        "p (e t) -> p e t", e=ET), ACT.Copy).then_inc(s["halo_done"], 1)
                else:
                    act.wait_ge(s["dl_done"], g)
                    act.wait_ge(s["halo_set"], g)
                    act.activation(xb[:, :, 0:TAPS - 1], halo[:], ACT.Copy).then_inc(s["halo_done"], 1)

            def xnT_scale(g, c, cc):
                act.wait_ge(s["xT_done"], g + 1)
                for k in range(DK):
                    act.activation(xnT[:, k, :], pT[:, k * TC:(k + 1) * TC], ACT.Copy,
                                   scale=prm[:, P_NORM + k:P_NORM + k + 1]).then_inc(s["xnT_done"], 1)

            def xb_copy(i):
                def f(g, c, cc):
                    slot = (PROJ * c + i) % 2
                    act.wait_ge(s["proj_done"], PROJ * g + i + 1)
                    act.activation(xb[:, 2 * i:2 * i + 2, TAPS - 1:TAPS - 1 + TC], pp[slot][:], ACT.Copy
                                   ).then_inc(s["proj_read"], 1)
                return f

            def z_silu(i):
                def f(g, c, cc):
                    q, slot = c % 2, (PROJ * c + 2 + i) % 2
                    if i == 0 and c:
                        act.wait_ge(s["gate_done"], g - 1)
                    act.wait_ge(s["proj_done"], PROJ * g + 3 + i)
                    act.activation(sz[q][:, 2 * i:2 * i + 2, :], pp[slot][:], ACT.Silu
                                   ).then_inc(s["proj_read"], 1)
                return f

            def conv_first(g, c, cc):
                act.wait_ge(s["proj_read"], PROJ * g + 2)
                act.wait_ge(s["halo_done"], g + 1)
                act.activation(halo[:], xb[:, :, TC:TC + TAPS - 1], ACT.Copy).then_inc(s["halo_set"], 1)
                for e in range(ET):
                    act.activation(t1[:, e, :], xb[:, e, 0:TC], ACT.Identity,
                                   scale=prm[:, P_CW + e * TAPS:P_CW + e * TAPS + 1],
                                   bias=prm[:, P_CB + e:P_CB + e + 1]).then_inc(s["tap0_done"], 1)

            def xc_silu(g, c, cc):
                q = c % 2
                act.wait_ge(s["tap_done"], ET * (TAPS - 1) * (g + 1))
                if c:
                    act.wait_ge(s["ydp_done"], ET * (g - 1))
                act.activation(xc[q][:], t1, ACT.Silu).then_inc(s["xc_done"], 1)

            def dbc_copy(g, c, cc):
                slot = (PROJ * c + 4) % 2
                act.wait_ge(s["proj_done"], PROJ * g + 5)
                if c:
                    act.wait_ge(s["c_stored"], 16 * g)
                act.activation(dbc[:], pp[slot][0:DBC, 0, :], ACT.Copy).then_inc(s["proj_read"], 1)

            def softplus_in(g, c, cc):
                q = c % 2
                if c:
                    act.wait_ge(s["exp_done"], ET * (g - 1))
                act.wait_ge(s["xc_done"], g + 1)
                for i in range(2):
                    slot = (PROJ * c + 5 + i) % 2
                    act.wait_ge(s["proj_done"], PROJ * g + 6 + i)
                    for e in range(2):
                        et = 2 * i + e
                        bias = prm[:, P_DTB + et:P_DTB + et + 1]
                        act.activation(t1[:, et, :], pp[slot][:, e, :], ACT.Abs, bias=bias)
                        last = act.activation(dl[q][:, et, :], pp[slot][:, e, :], ACT.Relu, bias=bias)
                    last.then_inc(s["proj_read"], 1)
                load_exp_ln(nc, act)
                act.wait_ge(s["proj_read"], PROJ * (g + 1))
                act.activation(t1, t1, ACT.Exp, scale=-1.0).then_inc(s["exp_neg_done"], 1)
                act.wait_ge(s["exp_neg_done"], g + 1)
                act.activation(t3, t1, ACT.Identity, bias=one_col[:, 0:1]).then_inc(s["one_plus_done"], 1)

            def softplus_ln(g, c, cc):
                act.wait_ge(s["sum_done"], g + 1)
                act.wait_ge(s["one_plus_done"], g + 1)
                act.activation(t1, t3, ACT.Ln).then_inc(s["ln_done"], 1)

            def ut_copy(b):
                def f(g, c, cc):
                    q = c % 2
                    if b == 0 and c:
                        act.wait_ge(s["v_done"], NU * (g - 1))
                    act.wait_ge(s["uT_done"], NB * g + b + 1)
                    act.activation(ut[q][b][0:BT, :], pT[0:BT, :], ACT.Copy).then_inc(s["ut_done"], 1)
                return f

            def carry_copy(b):
                def f(g, c, cc):
                    q = c % 2
                    act.wait_ge(s["carry_done"], NB * g + b + 1)
                    if b < NB - 1:
                        dst = ut[q][b + 1]
                    else:
                        dst = ut[1 - q][0]
                        if c:
                            act.wait_ge(s["v_done"], NU * (g - 1) + 2 * NB + 2)
                    act.activation(dst[BT:BT + N, :], pC[0:N, :], ACT.Copy).then_inc(s["carry_read"], 1)
                return f

            def exps(et, n0, n1):
                def f(g, c, cc):
                    q = c % 2
                    if n0 == 0:
                        act.wait_ge(s["dl_done"], g + 1)
                        if c:
                            last = (et // 2) * 2 * NB + 2 * (NB - 1) + et % 2
                            act.wait_ge(s["scan_done"], NU * (g - 1) + last + 1)
                    for n in range(n0, n1):
                        ins_ = act.activation(da[et][:, :, n, :], dl[q][:, et, :].rearrange(
                            "p (b t) -> p b t", b=NB), ACT.Exp, scale=rate[:, et, n:n + 1])
                    if n1 == N:
                        ins_.then_inc(s["exp_done"], 1)
                        act.wait_ge(s["exp_done"], ET * g + et + 1)
                        act.activation(a0[et][:], da[et][:, :, :, 0], ACT.Copy).then_inc(s["a0_copied"], 1)
                        act.wait_ge(s["a0_copied"], ET * g + et + 1)
                        act.activation(da[et][:, :, :, 0], zcol[:].rearrange("p (b n) -> p b n", b=NB),
                                       ACT.Copy).then_inc(s["a_done"], 1)
                return f

            def square(g, c, cc):
                act.wait_ge(s["xo_done"], g + 1)
                for j in range(TJ):
                    i = act.activation(y[c % 2][:, j, :], xo[:, j, :], ACT.Square,
                                       accum_out=ssq[:, bass.ds(cc * TJ + j, 1)])
                i.then_inc(s["sq_done"], 1)

            def front(g, c, cc):
                for f in (xnT_scale, halo_front, xb_copy(0), xb_copy(1), conv_first, z_silu(0), z_silu(1),
                          xc_silu, dbc_copy, softplus_in, softplus_ln):
                    f(g, c, cc)
                for b in range(NB):
                    ut_copy(b)(g, c, cc)
                    exps(0, b * (N // NB), (b + 1) * (N // NB))(g, c, cc)
                    carry_copy(b)(g, c, cc)
                exps(1, 0, N)(g, c, cc)

            items = [(0, "own", exps(2, 0, 8)),
                     (1, "front", xnT_scale),
                     (1, "own", exps(2, 8, N)),
                     (2, "front", halo_front),
                     (2, "front", xb_copy(0)),
                     (3, "own", exps(3, 0, 4)),
                     (3, "front", xb_copy(1)),
                     (3, "front", conv_first),
                     (4, "own", exps(3, 4, 8)),
                     (4, "front", z_silu(0)),
                     (4, "front", z_silu(1)),
                     (5, "front", xc_silu),
                     (6, "own", exps(3, 8, N)),
                     (6, "front", dbc_copy),
                     (7, "front", softplus_in),
                     (8, "back", square),
                     (8, "front", softplus_ln),
                     (12, "front", exps(0, 0, 8)),
                     (12, "front", exps(0, 8, N)),
                     (12, "front", ut_copy(0)),
                     (12, "front", exps(1, 0, 8)),
                     (12, "front", carry_copy(0)),
                     (12, "front", ut_copy(1)),
                     (12, "front", carry_copy(1)),
                     (12, "front", ut_copy(2)),
                     (12, "front", carry_copy(2)),
                     (12, "front", ut_copy(3)),
                     (12, "front", exps(1, 8, N)),
                     (12, "front", carry_copy(3))]

            def main(g, c, cc):
                for slot, kind, f in items:
                    if kind == "own":
                        f(g, c, cc)
                    elif kind == "front" and c != NC - 1:
                        f(g + 1, c + 1, cc + 1)
                    elif kind == "back" and c:
                        f(g - 1, c - 1, cc - 1)

            layers(act, prologue, front, main, square)

        @block.tensor
        def _(pe):
            pe.wait_ge(s["const_loaded"], 16 * (2 + 2 * NB))
            pe.wait_ge(s["padded"], 2 * NB)

            def prologue(l):
                pe.wait_ge(s["w_loaded"], W_ALL * (l + 1))
                pe.wait_ge(s["zeroed"], 3 * l + 4)

            def x_transpose(g, c, cc):
                pe.wait_ge(s["xn_done"], g + 1)
                if c:
                    pe.wait_ge(s["ut_done"], NB * g)
                for k in range(DK):
                    for j in range(TJ):
                        i = pe.transpose(pT[:, k * TC + j * P:k * TC + (j + 1) * P],
                                         x_in[:, j, k * P:(k + 1) * P], ident[:])
                i.then_inc(s["xT_done"], 1)

            def proj_slot(g, c, i):
                n = PROJ * g + i - 1
                if c or i >= 2:
                    pe.wait_ge(s["proj_read"], n)
                return (PROJ * c + i) % 2

            def in_proj(i):
                def f(g, c, cc):
                    slot = proj_slot(g, c, i)
                    if i == 0:
                        pe.wait_ge(s["xnT_done"], DK * (g + 1))
                    for e in range(2):
                        m = (2 * i + e) * P
                        for k in range(DK):
                            mm = pe.matmul(pp[slot][:, e, :], w_in[:, k, m:m + P], xnT[:, k, :],
                                           start=(k == 0), stop=(k == DK - 1))
                    mm.then_inc(s["proj_done"], 1)
                return f

            def x_proj(g, c, cc):
                q, slot = c % 2, proj_slot(g, c, 4)
                pe.wait_ge(s["xc_done"], g + 1)
                for e in range(ET):
                    mm = pe.matmul(pp[slot][0:DBC, 0, :], w_xp[:, e, :], xc[q][:, e, :],
                                   start=(e == 0), stop=(e == ET - 1))
                mm.then_inc(s["proj_done"], 1)

            def dt_proj(g, c, cc):
                pe.wait_ge(s["proj_read"], PROJ * g + 5)
                for i in range(2):
                    slot = proj_slot(g, c, 5 + i)
                    for e in range(2):
                        m = (2 * i + e) * P
                        mm = pe.matmul(pp[slot][:, e, :], w_dt[:, m:m + P], dbc[:],
                                       start=True, stop=True)
                    mm.then_inc(s["proj_done"], 1)

            def b_transpose(g, c, cc):
                if c:
                    pe.wait_ge(s["carry_read"], NB * g)
                    pe.wait_ge(s["xo_done"], g - 1)
                    take_waits(pe, s["waited_pe"])
                for b in range(NB):
                    mm = pe.transpose(pC[0:BT, b * DBC:(b + 1) * DBC], dbc[:, b * BT:(b + 1) * BT],
                                      ident[0:DBC, 0:DBC])
                mm.then_inc(s["bT_done"], 1)

            def u_transpose(b):
                def f(g, c, cc):
                    if b == 0:
                        pe.wait_ge(s["u_done"], g + 1)
                        pe.wait_ge(s["xnT_done"], DK * (g + 1))
                    else:
                        pe.wait_ge(s["ut_done"], NB * g + b)
                    take_waits(pe, s["waited_pe"])
                    for e in range(ET):
                        mm = pe.transpose(pT[0:BT, e * P:(e + 1) * P], t1[:, e, b * BT:(b + 1) * BT],
                                          ident[:])
                    mm.then_inc(s["uT_done"], 1)
                return f

            def carry(b):
                def f(g, c, cc):
                    q = c % 2
                    pe.wait_ge(s["moving_done"], NB * (g + 1))
                    pe.wait_ge(s["ut_done"], NB * g + b + 1)
                    if c or b:
                        pe.wait_ge(s["carry_read"], NB * g + b)
                    pe.matmul(pC[0:N, :], mv[q][b][:, :, BT - 1], ut[q][b][:], start=True, stop=True
                              ).then_inc(s["carry_done"], 1)
                return f

            def v_unit(g, c, u):
                q = c % 2
                _, b, _, et = unit(u)
                if c or u >= 2:
                    pe.wait_ge(s["scan_done"], NU * g + u - 1)
                if u == 0 and c == 0:
                    pe.wait_ge(s["carry_read"], NB * (g + 1))
                for h in range(N // HN):
                    mm = pe.matmul(pv[u % 2][:, h * HN:(h + 1) * HN, :], ut[q][b][:, et * P:(et + 1) * P],
                                   mv[q][b][:, h * HN:(h + 1) * HN, :], start=True, stop=True)
                mm.then_inc(s["v_done"], 1)

            def out_proj(g, c, cc):
                q = c % 2
                pe.wait_ge(s["gate_done"], g + 1)
                for j in range(TJ):
                    for e in range(ET):
                        mm = pe.matmul(pC[:, j * D:(j + 1) * D], y[q][:, e, j * P:(j + 1) * P],
                                       w_out[:, e, :], start=(e == 0), stop=(e == ET - 1))
                mm.then_inc(s["out_done"], 1)

            def out_proj_main(g, c, cc):
                pe.wait_ge(s["carry_read"], NB * (g + 2))
                out_proj(g, c, cc)

            def front(g, c, cc):
                for f in (x_transpose, in_proj(0), in_proj(1), in_proj(2), in_proj(3), x_proj, dt_proj,
                          b_transpose):
                    f(g, c, cc)
                for b in range(NB):
                    u_transpose(b)(g, c, cc)
                    carry(b)(g, c, cc)

            items = [(1, "front", x_transpose),
                     (3, "front", in_proj(0)),
                     (3, "front", in_proj(1)),
                     (4, "front", in_proj(2)),
                     (5, "front", in_proj(3)),
                     (6, "back", out_proj_main),
                     (6, "front", x_proj),
                     (8, "front", dt_proj),
                     (8, "front", b_transpose),
                     (12, "front", u_transpose(0)),
                     (13, "front", carry(0)),
                     (13, "front", u_transpose(1)),
                     (14, "front", carry(1)),
                     (14, "front", u_transpose(2)),
                     (15, "front", carry(2)),
                     (15, "front", u_transpose(3)),
                     (15, "front", carry(3))]

            def main(g, c, cc):
                table = slots(items, g, c, cc)
                for u in range(NU):
                    for f in table.get(u, []):
                        f()
                    v_unit(g, c, u)

            def post(g, c, cc):
                pe.wait_ge(s["xo_done"], g)
                out_proj(g, c, cc)

            layers(pe, prologue, front, main, post)

        @block.vector
        def _(dve):
            dve.memset(eps_col[:], EPS)
            dve.memset(one_col[:], 1.0)
            dve.memset(zcol[:], 0.0).then_inc(s["zeroed"], 1)
            dve.wait_ge(s["x0_loaded1"], 16)
            dve.tensor_tensor(x_all[1], x_all[1], x_all[1], ALU.mult).then_inc(s["squared"], 1)
            dve.wait_ge(s["squared"], 1)
            dve.tensor_reduce(ssq[:, TT // 2:TT], x_all[1], AXX, ALU.add).then_inc(s["ssq_done"], 1)

            def prologue(l):
                dve.wait_ge(s["sqrt_done"], l + 1)
                dve.reciprocal(rstd[:], rstd[:]).then_inc(s["rstd_done"], 1)
                dve.wait_ge(s["padded"], 2 * NB)
                dve.memset(ut[0][0][BT:KV, :], 0.0).then_inc(s["zeroed"], 1)
                dve.memset(first[:], 0.0).then_inc(s["zeroed"], 1)
                dve.memset(hlast[:], 0.0).then_inc(s["zeroed"], 1)
                dve.wait_ge(s["rstd_done"], l + 1)
                dve.wait_ge(s["zeroed"], 3 * l + 4)

            def x_norm(g, c, cc):
                dve.wait_ge(s["x_loaded"], 16 * (g + 1))
                for j in range(TJ):
                    i = dve.tensor_scalar(x_in[:, j, :], x_in[:, j, :], rstd[:, bass.ds(cc * TJ + j, 1)],
                                          None, ALU.mult)
                i.then_inc(s["xn_done"], 1)

            def conv(g, c, cc):
                for k in range(1, TAPS):
                    for e in range(ET):
                        n = ET * (TAPS - 1) * g + ET * (k - 1) + e
                        if k == 1:
                            dve.wait_ge(s["tap0_done"], ET * g + e + 1)
                        else:
                            dve.wait_ge(s["tap_done"], n - ET + 1)
                        w = P_CW + e * TAPS + k
                        dve.scalar_tensor_tensor(t1[:, e, :], xb[:, e, k:k + TC], prm[:, w:w + 1],
                                                 t1[:, e, :], ALU.mult, ALU.add).then_inc(s["tap_done"], 1)

            def step_size(g, c, cc):
                q = c % 2
                dve.wait_ge(s["ln_done"], g + 1)
                dve.scalar_tensor_tensor(t3, t3, -1.0, t1, ALU.add, ALU.subtract
                                         ).then_inc(s["correction_done"], 1)
                dve.wait_ge(s["correction_done"], g + 1)
                dve.scalar_tensor_tensor(dl[q][:], t3, 0.0, dl[q][:], ALU.max, ALU.subtract
                                         ).then_inc(s["dl_done"], 1)
                dve.wait_ge(s["dl_done"], g + 1)
                dve.scalar_tensor_tensor(t1, dl[q][:], -U_FLOOR, xc[q][:], ALU.min, ALU.mult
                                         ).then_inc(s["u_done"], 1)

            def moving(b):
                def f(g, c, cc):
                    q = c % 2
                    if b == 0:
                        dve.wait_ge(s["bT_done"], g + 1)
                        if c:
                            dve.wait_ge(s["v_done"], NU * (g - 1))
                    bT = pC[0:BT, b * DBC + B_ROW:b * DBC + B_ROW + N]
                    dve.tensor_tensor(mv[q][b][0:BT, :, :],
                                      tri[:].rearrange("p (o t) -> p o t", o=1).broadcast_to([BT, N, BT]),
                                      bT.rearrange("p (n o) -> p n o", o=1).broadcast_to([BT, N, BT]),
                                      ALU.mult).then_inc(s["moving_done"], 1)
                return f

            def sum_n(g, c, u):
                q = c % 2
                _, b, _, et = unit(u)
                if u == 0 and c:
                    dve.wait_ge(s["out_done"], g - 1)
                    dve.wait_ge(s["sq_done"], g - 1)
                dve.wait_ge(s["p_done"], NU * g + u + 1)
                dve.tensor_reduce(y[q][:, et, b * BT:(b + 1) * BT],
                                  ht[u % RING][:].rearrange("p (n t) -> p t n", n=N),
                                  AXX, ALU.add).then_inc(s["y_done"], 1)

            def scan_unit(g, c, u):
                _, b, e, et = unit(u)
                h = ht[u % RING]
                a = da[et][:, b, :, :].rearrange("p n t -> p (n t)")
                if b == 0:
                    dve.wait_ge(s["a_done"], ET * g + et + 1)
                    if c:
                        dve.wait_ge(s["h_done"], NU * (g - 1) + (et // 2) * 2 * NB + 2 * (NB - 1) + e + 1)
                    dve.tensor_tensor(first[:, et, :], a0[et][:, 0, :], hlast[:, et, :], ALU.mult
                                      ).then_inc(s["first_done"], 1)
                    dve.wait_ge(s["first_done"], ET * g + et + 1)
                else:
                    dve.wait_ge(s["h_done"], NU * g + u - 1)
                dve.wait_ge(s["v_done"], NU * g + u + 1)
                v0 = pv[u % 2][:, :, 0]
                dve.tensor_tensor(v0, v0, first[:, et, :], ALU.add).then_inc(s["add_done"], 1)
                dve.wait_ge(s["add_done"], NU * g + u + 1)
                if c or u >= RING:
                    dve.wait_ge(s["y_done"], NU * g + u - RING + 1)
                dve.tensor_tensor_scan(h[:], a, pv[u % 2][:].rearrange("p n t -> p (n t)"), 0.0,
                                       ALU.mult, ALU.add).then_inc(s["scan_done"], 1)
                dve.wait_ge(s["scan_done"], NU * g + u + 1)
                h_end = h[:].rearrange("p (n t) -> p n t", n=N)[:, :, BT - 1]
                if b < NB - 1:
                    dve.tensor_tensor(first[:, et, :], a0[et][:, b + 1, :], h_end, ALU.mult
                                      ).then_inc(s["h_done"], 1)
                else:
                    dve.tensor_copy(hlast[:, et, :], h_end).then_inc(s["h_done"], 1)

            def skip_term(g, c, cc):
                q = c % 2
                dve.wait_ge(s["y_done"], NU * (g + 1))
                for e in range(ET):
                    dve.scalar_tensor_tensor(y[q][:, e, :], xc[q][:, e, :], prm[:, P_DP + e:P_DP + e + 1],
                                             y[q][:, e, :], ALU.mult, ALU.add).then_inc(s["ydp_done"], 1)

            def residual(g, c, cc):
                dve.wait_ge(s["out_done"], g + 1)
                dve.wait_ge(s["xo_loaded"], 16 * (g + 1))
                dve.tensor_tensor(xo[:], pC[:].rearrange("p (j d) -> p j d", j=TJ), xo[:], ALU.add
                                  ).then_inc(s["xo_done"], 1)

            def front(g, c, cc):
                x_norm(g, c, cc)
                conv(g, c, cc)
                step_size(g, c, cc)
                for b in range(NB):
                    moving(b)(g, c, cc)

            items = [(0, "front", x_norm),
                     (2, "back", skip_term),
                     (4, "front", conv),
                     (6, "back", residual),
                     (9, "front", moving(0)),
                     (9, "front", step_size),
                     (10, "front", moving(1)),
                     (11, "front", moving(2)),
                     (11, "front", moving(3))]

            def main(g, c, cc):
                table = slots(items, g, c, cc)
                for u in range(NU):
                    for f in table.get(u, []):
                        f()
                    scan_unit(g, c, u)
                    if u >= 2:
                        sum_n(g, c, u - 2)
                    elif c:
                        sum_n(g - 1, c - 1, NU - 2 + u)

            def post(g, c, cc):
                sum_n(g, c, NU - 2)
                sum_n(g, c, NU - 1)
                skip_term(g, c, cc)
                residual(g, c, cc)

            layers(dve, prologue, front, main, post)

        @block.gpsimd
        def _(pool):
            for q in range(2):
                for b in range(NB):
                    pool.memset(ut[q][b][BT:KV, :], 0.0).then_inc(s["padded"], 1)
            pool.wait_ge(s["x_loaded"], 16)
            pool.wait_ge(s["x_copied"], 16)
            pool.dma_start(seq[2 * TC:T, :], ins["x"][2 * TC:T, :]).then_inc(s["rest_copied"], 16)

            def step_size(g, c, cc):
                q = c % 2
                pool.wait_ge(s["exp_neg_done"], g + 1)
                pool.tensor_tensor(dl[q][:], dl[q][:], t1, ALU.add).then_inc(s["sum_done"], 1)

            def times_c(g, c, u):
                _, b, _, _ = unit(u)
                h = ht[u % RING]
                pool.wait_ge(s["h_done"], NU * g + u + 1)
                if u < 2 * NB:
                    pool.wait_ge(cb_loaded[b], 16 * (g + 1))
                pool.tensor_tensor(h[:], h[:], cb[:, b, :], ALU.mult).then_inc(s["p_done"], 1)

            def gate(g, c, cc):
                q = c % 2
                pool.wait_ge(s["ydp_done"], ET * (g + 1))
                pool.wait_ge(s["proj_read"], PROJ * g + 4)
                pool.tensor_tensor(y[q][:], y[q][:], sz[q][:], ALU.mult).then_inc(s["gate_done"], 1)

            items = [(2, "back", gate),
                     (8, "front", step_size)]

            def main(g, c, cc):
                table = slots(items, g, c, cc)
                for u in range(NU):
                    for f in table.get(u, []):
                        f()
                    times_c(g, c, u)

            layers(pool, lambda l: None, step_size, main, gate)


def build_experts(nc, ins, x0, x2, out):
    with ExitStack() as ctx:
        def sb(name, shape, dt=F32):
            return ctx.enter_context(nc.sbuf_tensor(name, shape, dt))

        def ps(name, shape, dt=F32):
            return ctx.enter_context(nc.psum_tensor(name, shape, dt))

        def sem(name):
            return ctx.enter_context(nc.semaphore("m_" + name))

        table = nc.dram_tensor("x1_table", [T, D], F32, kind="Internal").ap()
        total = nc.dram_tensor("x1_total", [T, D], F32, kind="Internal").ap()
        ET_ = NX * TT

        ident = sb("ident2", [P, P])
        upper = sb("upper", [P, P])
        ones = sb("ones", [P, P])
        iota = sb("iota", [P, P])
        place = sb("place", [P, TT, 2])
        w_ch = sb("w_ch", [P, DK, NX])
        eps2 = sb("eps2", [P, 1])
        xa = [sb(f"xa{q}", [P, GRP, D]) for q in range(2)]
        xb2 = [sb(f"xb2{q}", [P, GRP, D]) for q in range(2)]
        stats = sb("stats", [P, GRP, 6])
        mv_ = sb("mv_", [P, GRP, 2])
        rs = sb("rs", [P, GRP])
        xT = [sb(f"xT{i}", [P, 2, DK, P]) for i in range(2)]
        logit = sb("logit", [P, TT, NX])
        prob = sb("prob", [P, NX, TT])
        rowmax = sb("rowmax", [P, TT])
        rowsum = sb("rowsum", [P, TT])
        thr = sb("thr", [P, NX], U32)
        cand = sb("cand", [P, DIG, NX], U32)
        digit = sb("digit", [P, DIG, NX], U32)
        inc = sb("inc", [P, DIG, NX], U32)
        best = sb("best", [P, NX], U32)
        cnt = sb("cnt", [P, DIG, NX])
        reach = sb("reach", [P, DIG, NX, TT])
        need = sb("need", [P, NX])
        ge = sb("ge", [P, NX, TT])
        gt = sb("gt", [P, NX, TT])
        same = sb("same", [P, NX, TT])
        rank = sb("rank", [P, NX, TT])
        again = sb("again", [P, NX, TT])
        slot = sb("slot", [P, NX, TT], U32)
        slot_g = sb("slot_g", [P, NX, TT], U32)
        slot_p = sb("slot_p", [P, NX, TT], U32)
        hot_g = sb("hot_g", [P, ET_, CG], BF16)
        val = sb("val", [P, ET_, VALS], BF16)
        rest = sb("rest", [P, ET_])
        hot_val = sb("hot_val", [P, ET_, CG, VALS], BF16)
        hot_p = [sb(f"hot_p{i}", [P, TT, P], BF16) for i in range(2)]
        lists = sb("lists", [P, NX, CG, VALS])
        token = sb("token", [P, NX, CG], U32)
        gate = sb("gate", [P, NX, CG])
        token_e = [sb(f"token_e{q}", [P, CG], U32) for q in range(2)]
        gate_e = [sb(f"gate_e{q}", [P, CG]) for q in range(2)]
        w1 = [sb(f"w1{q}", [P, DK, F]) for q in range(2)]
        w2 = [sb(f"w2{q}", [P, FK, D]) for q in range(2)]
        xe = [xa[q] for q in range(2)]
        oe = [xb2[q] for q in range(2)]
        xeT = sb("xeT", [P, DK, CAP])
        hT = sb("hT", [P, FK, CAP])

        pX = [ps(f"pX{i}", [P, 2, DK, P]) for i in range(2)]
        pH = [ps(f"pH{i}", [P, 512]) for i in range(2)]
        pY = [ps(f"pY{i}", [P, 2, D]) for i in range(2)]
        pR = ps("pR", [P, 2, NX * TT])
        pN = ps("pN", [P, 512])

        names = (
            "const", "xin0", "xin1", "add", "stat", "aggr", "sqrt", "recip", "x1", "x1_kept",
            "xT_ps", "xT_sb", "logit_ps", "logit_sb", "centred", "expd", "chain", "cnt", "tot",
            "eq", "ranked", "hot", "listed", "weights0", "weights1", "chosen", "gathered0",
            "gathered1", "xeT_ps", "xeT_sb", "h_ps", "h_sb", "y_ps", "gated", "added", "fin_in0",
            "fin_in1", "out", "eps", "total_set", "waited_sp", "waited_pool")
        s = {n: sem(n) for n in names}
        block = ctx.enter_context(nc.Block())

        def rows(ap, k, tiles):
            return ap[bass.ds(k * (tiles * P), tiles * P), :].rearrange("(j p) d -> p j d", p=P)

        def pairs(eng, n, f):
            with eng.Fori(0, n // 2) as i:
                for q in range(2):
                    f(2 * i + q, q, i)

        @block.sync
        def _(sp):
            for t, n in ((ident, "ident"), (upper, "upper"), (ones, "ones"), (iota, "iota"),
                         (place, "place"), (w_ch, "w_ch"), (digit, "digit"), (again, "again")):
                sp.dma_start(t[:], ins[n]).then_inc(s["const"], 16)

            def load(k, q, i):
                sp.dma_start(xa[q][:], rows(x0, k, GRP)).then_inc(s[f"xin{q}"], 16)
                sp.dma_start(xb2[q][:], rows(x2, k, GRP)).then_inc(s[f"xin{q}"], 16)

            for q in range(2):
                load(q, q, 0)

            def keep(k):
                sp.wait_ge(s["x1"], k + 1)
                sp.dma_start(rows(table, k, GRP), xa[k % 2][:]).then_inc(s["x1_kept"], 16)

            for k in range(NG):
                keep(k)
                if k + 2 < NG:
                    sp.wait_ge(s["x1_kept"], 16 * (k + 1))
                    sp.wait_ge(s["xT_ps"], GRP // 2 * (k + 1))
                    load(k + 2, k % 2, 0)

            sp.wait_ge(s["x1_kept"], 16 * NG)
            sp.dma_start(total, table).then_inc(s["total_set"], 16)

            for q in range(2):
                sp.dma_start(w1[q][:], ins["w1"][q]).then_inc(s[f"weights{q}"], 16)
                sp.dma_start(w2[q][:], ins["w2"][q]).then_inc(s[f"weights{q}"], 16)
            with sp.Fori(1, NX // 2) as i:
                for q in range(2):
                    sp.wait_ge(s["y_ps"], CG // 2 * (2 * i + q - 1))
                    take_waits(sp, s["waited_sp"])
                    e = 2 * i + q
                    sp.dma_start(w1[q][:], ins["w1"][bass.ds(e, 1)].rearrange("a p k n -> p (a k) n")
                                 ).then_inc(s[f"weights{q}"], 16)
                    sp.dma_start(w2[q][:], ins["w2"][bass.ds(e, 1)].rearrange("a p k n -> p (a k) n")
                                 ).then_inc(s[f"weights{q}"], 16)

            sp.wait_ge(s["added"], 16 * CG * NX)
            for q in range(2):
                sp.dma_start(xa[q][:], rows(total, q, GRP)).then_inc(s[f"fin_in{q}"], 16)
            for k in range(NG):
                sp.wait_ge(s["x1"], NG + k + 1)
                sp.dma_start(rows(out, k, GRP), xa[k % 2][:]).then_inc(s["out"], 16)
                if k + 2 < NG:
                    sp.wait_ge(s["out"], 16 * (k + 1))
                    sp.dma_start(xa[k % 2][:], rows(total, k + 2, GRP)).then_inc(s[f"fin_in{k % 2}"], 16)
            sp.wait_ge(s["out"], 16 * NG)

        @block.scalar
        def _(act):
            act.wait_ge(s["eps"], 1)

            def std(k):
                act.wait_ge(s["aggr"], GRP * (k + 1))
                if k:
                    act.wait_ge(s["x1"], k)
                act.activation(rs[:], mv_[:, :, 1], ACT.Sqrt, bias=eps2[:, 0:1]).then_inc(s["sqrt"], 1)

            for k in range(NG):
                std(k)
                for i in range(GRP // 2):
                    n = k * (GRP // 2) + i
                    act.wait_ge(s["xT_ps"], n + 1)
                    if n >= 2:
                        act.wait_ge(s["logit_ps"], 2 * (n - 1))
                    act.activation(xT[n % 2][:], pX[n % 2][:], ACT.Copy).then_inc(s["xT_sb"], 1)
                act.wait_ge(s["logit_ps"], GRP * (k + 1))
                act.activation(logit[:, k * GRP:(k + 1) * GRP, :],
                               pN[:, 0:GRP * NX].rearrange("p (j e) -> p j e", e=NX), ACT.Copy
                               ).then_inc(s["logit_sb"], 1)
            act.wait_ge(s["centred"], 1)
            act.activation(logit[:], logit[:], ACT.Exp).then_inc(s["expd"], 1)

            def expert(e, q, i):
                for j in range(CG // 2):
                    n = e * (CG // 2) + j
                    act.wait_ge(s["xeT_ps"], n + 1)
                    if j == 0:
                        act.wait_ge(s["h_ps"], e * (2 * FK))
                    act.activation(xeT[:, :, 2 * j * P:(2 * j + 2) * P],
                                   pX[j % 2][:].rearrange("p a k c -> p (a k c)").rearrange(
                                       "p (k c) -> p k c", k=DK), ACT.Copy).then_inc(s["xeT_sb"], 1)
                for h in range(2):
                    for f in range(FK):
                        m = h * FK + f
                        act.wait_ge(s["h_ps"], e * (2 * FK) + m + 1)
                        if m == 0:
                            act.wait_ge(s["y_ps"], e * (CG // 2))
                        act.activation(hT[:, f, h * 512:(h + 1) * 512], pH[m % 2][:], ACT.Silu
                                       ).then_inc(s["h_sb"], 1)

            pairs(act, NX, expert)
            for k in range(NG):
                std(NG + k)

        @block.tensor
        def _(pe):
            pe.wait_ge(s["const"], 16 * 8)
            for k in range(NG):
                pe.wait_ge(s["x1"], k + 1)

                def logits(n):
                    pe.wait_ge(s["xT_sb"], n + 1)
                    if n % (GRP // 2) == 0 and n:
                        pe.wait_ge(s["logit_sb"], n // (GRP // 2))
                    for a in range(2):
                        t = (2 * n + a) % GRP
                        for c in range(DK):
                            mm = pe.matmul(pN[:, t * NX:(t + 1) * NX], xT[n % 2][:, a, c, :], w_ch[:, c, :],
                                           start=(c == 0), stop=(c == DK - 1))
                        mm.then_inc(s["logit_ps"], 1)

                for i in range(GRP // 2):
                    n = k * (GRP // 2) + i
                    if n >= 2:
                        pe.wait_ge(s["xT_sb"], n - 1)
                    for a in range(2):
                        for c in range(DK):
                            mm = pe.transpose(pX[n % 2][:, a, c, :], xa[k % 2][:, 2 * i + a, c * P:(c + 1) * P],
                                              ident[:])
                    mm.then_inc(s["xT_ps"], 1)
                    if i:
                        logits(n - 1)
                logits(k * (GRP // 2) + GRP // 2 - 1)
            pe.wait_ge(s["logit_sb"], NG)
            with pe.Fori(0, ROUNDS) as i:
                pe.wait_ge(s["cnt"], i + 1)
                pe.matmul(pN[:, 0:DIG * NX], ones[:], cnt[:].rearrange("p m e -> p (m e)"),
                          start=True, stop=True).then_inc(s["tot"], 1)
            pe.wait_ge(s["cnt"], ROUNDS + 1)
            pe.matmul(pN[:, 0:NX], ones[:], cnt[:, 0, :], start=True, stop=True).then_inc(s["tot"], 1)
            for n in range(2):
                src = (same, gt)[n]
                pe.wait_ge(s["eq"], n + 1)
                flat = src[:].rearrange("p e t -> p (e t)")
                pe.matmul(pR[:, 0, :], upper[:], flat, start=True, stop=True)
                pe.matmul(pR[:, 1, :], ones[:], flat, start=True, stop=True).then_inc(s["ranked"], 1)
            for e in range(NX):
                pe.wait_ge(s["hot"], e + 1)
                for t in range(TT):
                    mm = pe.matmul(pH[0][:, e * CG * VALS:(e + 1) * CG * VALS], hot_p[e % 2][:, t, :],
                                   hot_val[:, e * TT + t, :, :].rearrange("p g v -> p (g v)"),
                                   start=(t == 0), stop=(t == TT - 1))
                mm.then_inc(s["listed"], 1)

            def expert(e, q, i):
                for j in range(CG // 2):
                    if j == 0:
                        pe.wait_ge(s[f"gathered{q}"], i * (16 * CG) + 16 * CG)
                        pe.wait_ge(s[f"weights{q}"], i * 32 + 32)
                        pe.wait_ge(s["xeT_sb"], e * (CG // 2))
                    elif j >= 2:
                        pe.wait_ge(s["xeT_sb"], e * (CG // 2) + j - 1)
                    for c in range(DK):
                        for a in range(2):
                            flat = pX[j % 2][:].rearrange("p a k c -> p (a k c)")
                            mm = pe.transpose(flat[:, (2 * c + a) * P:(2 * c + a + 1) * P],
                                              xe[q][:, 2 * j + a, c * P:(c + 1) * P], ident[:])
                    mm.then_inc(s["xeT_ps"], 1)
                for h in range(2):
                    pe.wait_ge(s["xeT_sb"], e * (CG // 2) + 2 * (h + 1))
                    for f in range(FK):
                        m = h * FK + f
                        pe.wait_ge(s["h_sb"], e * (2 * FK) + m - 1) if m >= 2 else pe.wait_ge(
                            s["h_sb"], e * (2 * FK))
                        for c in range(DK):
                            mm = pe.matmul(pH[m % 2][:], w1[q][:, c, f * P:(f + 1) * P],
                                           xeT[:, c, h * 512:(h + 1) * 512],
                                           start=(c == 0), stop=(c == DK - 1))
                        mm.then_inc(s["h_ps"], 1)
                for j in range(CG // 2):
                    if j == 0 or j == 2:
                        pe.wait_ge(s["h_sb"], e * (2 * FK) + FK * (j // 2 + 1))
                    if j >= 2:
                        pe.wait_ge(s["gated"], e * CG + 2 * (j - 1))
                    else:
                        pe.wait_ge(s["gated"], e * CG)
                    for a in range(2):
                        g = 2 * j + a
                        for f in range(FK):
                            mm = pe.matmul(pY[j % 2][:, a, :], hT[:, f, g * P:(g + 1) * P], w2[q][:, f, :],
                                           start=(f == 0), stop=(f == FK - 1))
                    mm.then_inc(s["y_ps"], 1)

            pe.wait_ge(s["chosen"], 1)
            pairs(pe, NX, expert)

        @block.vector
        def _(dve):
            dve.memset(eps2[:], EPS).then_inc(s["eps"], 1)

            count = [0]

            def link(i):
                count[0] += 1
                i.then_inc(s["chain"], 1)
                dve.wait_ge(s["chain"], count[0])

            def normalise(k, q):
                if k:
                    dve.wait_ge(s["sqrt"], k)
                for j in range(GRP):
                    dve.bn_stats(stats[:, j, :], xa[q][:, j, :]).then_inc(s["stat"], 1)
                for j in range(GRP):
                    dve.wait_ge(s["stat"], GRP * k + j + 1)
                    dve.bn_aggr(mv_[:, j, :], stats[:, j, :]).then_inc(s["aggr"], 1)
                dve.wait_ge(s["sqrt"], k + 1)
                dve.reciprocal(rs[:], rs[:]).then_inc(s["recip"], 1)
                dve.wait_ge(s["recip"], k + 1)
                for j in range(GRP):
                    i = dve.tensor_scalar(xa[q][:, j, :], xa[q][:, j, :], mv_[:, j, 0:1], rs[:, j:j + 1],
                                          ALU.subtract, ALU.mult)
                i.then_inc(s["x1"], 1)
                dve.wait_ge(s["x1"], k + 1)

            for k in range(NG):
                q = k % 2
                dve.wait_ge(s[f"xin{q}"], 32 * (k // 2 + 1))
                dve.tensor_tensor(xa[q][:], xa[q][:], xb2[q][:], ALU.add).then_inc(s["add"], 1)
                dve.wait_ge(s["add"], k + 1)
                normalise(k, q)

            def over_e(v):
                return v.rearrange("p (t o) -> p t o", o=1).broadcast_to([P, TT, NX])

            dve.wait_ge(s["logit_sb"], NG)
            link(dve.tensor_reduce(rowmax[:], logit[:], AXX, ALU.max))
            dve.tensor_tensor(logit[:], logit[:], over_e(rowmax[:]), ALU.subtract).then_inc(s["centred"], 1)
            dve.wait_ge(s["expd"], 1)
            link(dve.tensor_reduce(rowsum[:], logit[:], AXX, ALU.add))
            link(dve.reciprocal(rowsum[:], rowsum[:]))
            link(dve.tensor_tensor(prob[:].rearrange("p e t -> p t e"), logit[:], over_e(rowsum[:]), ALU.mult))

            def per_e(v):
                return v.rearrange("p (e o) -> p e o", o=1).broadcast_to([P, NX, TT])

            dve.wait_ge(s["const"], 16 * 8)
            link(dve.memset(thr[:], 0))
            base, steps = count[0], 6
            with dve.Fori(0, ROUNDS) as i:
                def step(k, ins_):
                    ins_.then_inc(s["chain"], 1)
                    dve.wait_ge(s["chain"], i * steps + (base + k))

                step(1, dve.tensor_tensor(cand[:], thr[:].rearrange("p (o e) -> p o e", o=1)
                                          .broadcast_to([P, DIG, NX]), digit[:], ALU.bitwise_or))
                step(2, dve.tensor_tensor(reach[:], prob[:].rearrange("p (o e) t -> p o e t", o=1)
                                          .broadcast_to([P, DIG, NX, TT]),
                                          cand[:].bitcast(F32).rearrange("p m (e o) -> p m e o", o=1)
                                          .broadcast_to([P, DIG, NX, TT]), ALU.is_ge))
                dve.tensor_reduce(cnt[:], reach[:], AXX, ALU.add).then_inc(s["cnt"], 1)
                dve.wait_ge(s["tot"], i + 1)
                step(3, dve.scalar_tensor_tensor(inc[:], pN[:, 0:DIG * NX].rearrange("p (m e) -> p m e", m=DIG),
                                                 CAP - 0.5, digit[:], ALU.is_ge, ALU.mult))
                step(4, dve.tensor_reduce(best[:], inc[:].rearrange("p m e -> p e m"), AXX, ALU.max))
                step(5, dve.tensor_tensor(thr[:], thr[:], best[:], ALU.bitwise_or))
                step(6, dve.tensor_single_scalar(digit[:], digit[:], 2, ALU.logical_shift_right))
            count[0] = base + steps * ROUNDS

            dve.tensor_tensor(same[:], prob[:], per_e(thr[:].bitcast(F32)), ALU.is_equal).then_inc(s["eq"], 1)
            link(dve.tensor_tensor(gt[:], prob[:], per_e(thr[:].bitcast(F32)), ALU.is_gt))
            dve.tensor_reduce(cnt[:, 0, :], gt[:], AXX, ALU.add).then_inc(s["cnt"], 1)
            dve.wait_ge(s["tot"], ROUNDS + 1)
            link(dve.tensor_scalar(need[:], pN[:, 0:NX], -1.0, float(CAP), ALU.mult, ALU.add))

            def ranks(n):
                flat = rank[:].rearrange("p e t -> p (e t)")
                dve.wait_ge(s["ranked"], n + 1)
                link(dve.tensor_tensor_scan(flat, again[:].rearrange("p e t -> p (e t)"), pR[:, 1, :],
                                            0.0, ALU.mult, ALU.add))
                link(dve.tensor_tensor(flat, flat, pR[:, 1, :], ALU.subtract))
                link(dve.tensor_tensor(flat, flat, pR[:, 0, :], ALU.add))

            ranks(0)
            link(dve.tensor_tensor(ge[:], rank[:], per_e(need[:]), ALU.is_le))
            link(dve.tensor_tensor(ge[:], ge[:], same[:], ALU.mult))
            dve.tensor_tensor(gt[:], gt[:], ge[:], ALU.add).then_inc(s["eq"], 1)
            dve.wait_ge(s["eq"], 2)
            ranks(1)
            FAR = 8 * CAP
            link(dve.scalar_tensor_tensor(rank[:], rank[:], float(-1 - FAR), gt[:], ALU.add, ALU.mult))
            link(dve.tensor_scalar(slot[:], rank[:], float(FAR), None, ALU.add))
            dve.tensor_single_scalar(slot_g[:], slot[:], 7, ALU.logical_shift_right)
            link(dve.tensor_single_scalar(slot_p[:], slot[:], P - 1, ALU.bitwise_and))
            sg = slot_g[:].rearrange("p e (t o) -> p (e t) o", o=1).broadcast_to([P, ET_, CG])
            dve.tensor_tensor(hot_g[:], iota[:, 0:CG].rearrange("p (o g) -> p o g", o=1)
                              .broadcast_to([P, ET_, CG]), sg, ALU.is_equal)
            for e in range(NX):
                dve.tensor_copy(val[:, e * TT:(e + 1) * TT, 0:2], place[:])
            pf = prob[:].rearrange("p e t -> p (e t)")
            link(dve.tensor_copy(val[:, :, 2], pf))
            link(dve.tensor_tensor(rest[:], pf, val[:, :, 2], ALU.subtract))
            link(dve.tensor_copy(val[:, :, 3], rest[:]))
            link(dve.tensor_tensor(rest[:], rest[:], val[:, :, 3], ALU.subtract))
            link(dve.tensor_copy(val[:, :, 4], rest[:]))
            link(dve.tensor_tensor(
                hot_val[:], hot_g[:].rearrange("p c (g o) -> p c g o", o=1).broadcast_to([P, ET_, CG, VALS]),
                val[:].rearrange("p c (o v) -> p c o v", o=1).broadcast_to([P, ET_, CG, VALS]), ALU.mult))
            for e in range(NX):
                if e >= 2:
                    dve.wait_ge(s["listed"], e - 1)
                dve.tensor_tensor(hot_p[e % 2][:], iota[:].rearrange("p (o c) -> p o c", o=1)
                                  .broadcast_to([P, TT, P]),
                                  slot_p[:, e, :].rearrange("p (t o) -> p t o", o=1)
                                  .broadcast_to([P, TT, P]), ALU.is_equal).then_inc(s["hot"], 1)
            dve.wait_ge(s["listed"], NX)
            link(dve.tensor_copy(lists[:].rearrange("p e g v -> p (e g v)"), pH[0][:, 0:NX * CG * VALS]))
            link(dve.scalar_tensor_tensor(token[:], lists[:, :, :, 0], float(P), lists[:, :, :, 1],
                                          ALU.mult, ALU.add))
            link(dve.tensor_tensor(gate[:], lists[:, :, :, 2], lists[:, :, :, 3], ALU.add))
            dve.tensor_tensor(gate[:], gate[:], lists[:, :, :, 4], ALU.add).then_inc(s["chosen"], 1)
            dve.wait_ge(s["chosen"], 1)

            def choose(e, q):
                dve.tensor_copy(gate_e[q][:], gate[:, bass.ds(e, 1), :].rearrange("p a g -> p (a g)"))
                dve.tensor_copy(token_e[q][:], token[:, bass.ds(e, 1), :].rearrange("p a g -> p (a g)")
                                ).then_inc(s["chosen"], 1)

            choose(0, 0)

            def expert(e, q, i):
                dve.wait_ge(s["added"], e * (16 * CG))
                if q == 0:
                    choose(e + 1, 1)
                else:
                    dve.tensor_copy(gate_e[0][:], gate[:, bass.ds(nxt(i), 1), :].rearrange("p a g -> p (a g)"))
                    dve.tensor_copy(token_e[0][:], token[:, bass.ds(nxt(i), 1), :].rearrange(
                        "p a g -> p (a g)")).then_inc(s["chosen"], 1)
                for j in range(CG // 2):
                    dve.wait_ge(s["y_ps"], e * (CG // 2) + j + 1)
                    for a in range(2):
                        g = 2 * j + a
                        dve.tensor_scalar(oe[q][:, g, :], pY[j % 2][:, a, :], gate_e[q][:, g:g + 1], None,
                                          ALU.mult).then_inc(s["gated"], 1)

            def nxt(i):
                return i * 2 + 2

            with dve.Fori(0, NX // 2 - 1) as i:
                for q in range(2):
                    expert(2 * i + q, q, i)
            last = NX // 2 - 1
            expert(2 * last, 0, last)
            e = NX - 1
            for j in range(CG // 2):
                dve.wait_ge(s["y_ps"], e * (CG // 2) + j + 1)
                for a in range(2):
                    g = 2 * j + a
                    dve.tensor_scalar(oe[1][:, g, :], pY[j % 2][:, a, :], gate_e[1][:, g:g + 1], None,
                                      ALU.mult).then_inc(s["gated"], 1)

            for k in range(NG):
                dve.wait_ge(s[f"fin_in{k % 2}"], 16 * (k // 2 + 1))
                normalise(NG + k, k % 2)

        @block.gpsimd
        def _(pool):
            pool.wait_ge(s["x1_kept"], 16 * NG)

            def gather(e, q):
                pool.wait_ge(s["chosen"], e + 2)
                pool.wait_ge(s["xeT_ps"], (e - 1) * (CG // 2))
                take_waits(pool, s["waited_pool"])
                for g in range(CG):
                    pool.indirect_dma_start(xe[q][:, g, :], None, table, bass.IndirectOffsetOnAxis(
                        ap=token_e[q][:, g:g + 1], axis=0)).then_inc(s[f"gathered{q}"], 16)

            def scatter(e, q):
                pool.wait_ge(s["total_set"], 16)
                pool.wait_ge(s["added"], e * (16 * CG))
                for g in range(CG):
                    pool.wait_ge(s["gated"], e * CG + g + 1)
                    take_waits(pool, s["waited_pool"])
                    pool.indirect_dma_start(total, bass.IndirectOffsetOnAxis(
                        ap=token_e[q][:, g:g + 1], axis=0), oe[q][:, g, :], None,
                        compute_op=ALU.add).then_inc(s["added"], 16)

            pool.wait_ge(s["chosen"], 2)
            for g in range(CG):
                pool.indirect_dma_start(xe[0][:, g, :], None, table, bass.IndirectOffsetOnAxis(
                    ap=token_e[0][:, g:g + 1], axis=0)).then_inc(s["gathered0"], 16)
            with pool.Fori(0, NX // 2 - 1) as i:
                for q in range(2):
                    e = 2 * i + q
                    gather(e + 1, 1 - q)
                    scatter(e, q)
            gather(NX - 1, 1)
            scatter(NX - 2, 0)
            scatter(NX - 1, 1)


def kernel(**inputs):
    import numpy as np
    import concourse.bacc as bacc
    from concourse.bass_utils import run_bass_kernel_spmd

    a = {k: np.asarray(v) for k, v in inputs.items()}

    def tiles(w):
        return w.reshape(w.shape[0], -1, P, w.shape[2]).transpose(0, 2, 1, 3)

    x_proj = a["L0_attn_x_proj_w"].transpose(0, 2, 1)
    w_xp = np.zeros((NL, E, DBC), np.float32)
    for to, part in ((0, 0), (B_ROW, R), (C_ROW, R + N)):
        w_xp[:, :, to:to + N] = x_proj[:, :, part:part + N]
    w_dt = np.zeros((NL, DBC, E), np.float32)
    w_dt[:, 0:R, :] = a["L0_attn_dt_w"].transpose(0, 2, 1)
    per_channel = [a["L0_attn_norm_w"].reshape(NL, DK, P).transpose(0, 2, 1),
                   a["L0_attn_conv_w"].reshape(NL, ET, P, TAPS).transpose(0, 2, 1, 3).reshape(NL, P, -1)]
    per_channel += [a[k].reshape(NL, ET, P).transpose(0, 2, 1)
                    for k in ("L0_attn_conv_b", "L0_attn_dt_b", "L0_attn_Dp")]
    steps = np.arange(BT)
    lag = steps[None, :] - steps[:, None]
    carry = np.zeros((KV - BT, N, BT), np.float32)
    carry[np.arange(N), np.arange(N), :] = BETA ** (steps + 1.0)
    again = np.ones((P, NX, TT), np.float32)
    again[:, :, 0] = 0.0
    place = np.empty((P, TT, 2), np.float32)
    place[:, :, 0] = np.arange(TT)[None, :]
    place[:, :, 1] = np.arange(P)[:, None]
    arrays = {
        "x": a["L0_attn_x"][0],
        "w_in": tiles(a["L0_attn_in_proj_w"].transpose(0, 2, 1)),
        "w_out": tiles(a["L0_attn_out_w"].transpose(0, 2, 1)),
        "w_xp": tiles(w_xp),
        "w_dt": w_dt,
        "prm": np.concatenate(per_channel, axis=2),
        "a_log": a["L0_attn_A_log"].reshape(NL, ET, P, N).transpose(0, 2, 1, 3),
        "ident": np.eye(P, dtype=np.float32),
        "tri": np.where(lag >= 0, -BETA ** np.maximum(lag, 0).astype(np.float64), 0.0).astype(np.float32),
        "carry": carry,
        "upper": np.triu(np.ones((P, P), np.float32)),
        "ones": np.ones((P, P), np.float32),
        "iota": np.broadcast_to(np.arange(P, dtype=np.float32), (P, P)),
        "place": place,
        "digit": np.broadcast_to(((np.arange(DIG, dtype=np.uint32) + 1) << (BITS - 2))[None, :, None],
                                 (P, DIG, NX)),
        "again": again,
        "w_ch": a["L0_ffn_choice_w"].T.reshape(DK, P, NX).transpose(1, 0, 2),
        "w1": tiles(a["L0_ffn_w1"]),
        "w2": tiles(a["L0_ffn_w2"]),
    }
    arrays = {k: np.ascontiguousarray(v) for k, v in arrays.items()}
    nc = bacc.Bacc("TRN2", target_bir_lowering=False, num_devices=1)
    ins = {}
    for k, v in arrays.items():
        ins[k] = nc.dram_tensor("in_" + k, v.shape, mybir.dt.from_np(v.dtype), kind="ExternalInput").ap()
    out = nc.dram_tensor("out", [T, D], F32, kind="ExternalOutput").ap()
    seq = nc.dram_tensor("seq", [(NL + 1) * T, D], F32, kind="Internal").ap()
    build_mamba(nc, ins, seq)
    build_experts(nc, ins, ins["x"], seq[NL * T:(NL + 1) * T, :], out)
    r = run_bass_kernel_spmd(nc, [{"in_" + k: v for k, v in arrays.items()}], core_ids=[0])
    return r.results[0]["out"].reshape(1, T, D)
```
